# Optimizing a Trainium2 kernel written in Bass

```python
import numpy as np
import jax
import jax.numpy as jnp

def _softmax(x, axis=-1):
    return jax.nn.softmax(x, axis=axis)

def _gelu(x):
    return jax.nn.gelu(x, approximate=True)

def _silu(x):
    return jax.nn.silu(x)

def _sigmoid(x):
    return jax.nn.sigmoid(x)

def _layernorm(x, axis=-1, eps=1e-05):
    m = jnp.mean(x, axis=axis, keepdims=True)
    v = jnp.var(x, axis=axis, keepdims=True)
    return (x - m) / jnp.sqrt(v + eps)

def _scatter_add(tgt, idx, src, axis=0):
    return tgt.at[idx].add(src)

def _segment_sum(src, seg, n):
    return jax.ops.segment_sum(src, seg, n)
kernel_name = 'mk_seq_postln_d1_jaxref_r4_bffffa'

def setup_inputs(seed: int=0):
    np.random.seed(seed)
    _w = jnp.asarray

    def _L0_attn_setup():
        import jax, jax.numpy as jnp
        import numpy as np
        from jax import lax
        BLOCK_LEN = 128
        NEG_INF = -1000000000.0
        key = jax.random.key(seed)
        ks = jax.random.split(key, 8)
        N, L, Dm = (2, 2048, 1024)
        W, H, dh = (256, 16, 64)
        s = lambda fan: 1.0 / np.sqrt(fan)
        return {'inputs': jax.random.normal(ks[0], (N, L, Dm), jnp.float32), 'conv_w': jax.random.normal(ks[1], (3, Dm, 3 * W), jnp.float32) * s(3 * Dm), 'conv_b': jnp.zeros((3 * W,), jnp.float32), 'wq': jax.random.normal(ks[2], (W, H, dh), jnp.float32) * s(W), 'bq': jnp.zeros((H, dh), jnp.float32), 'wk': jax.random.normal(ks[3], (W, H, dh), jnp.float32) * s(W), 'bk': jnp.zeros((H, dh), jnp.float32), 'wv': jax.random.normal(ks[4], (W, H, dh), jnp.float32) * s(W), 'bv': jnp.zeros((H, dh), jnp.float32), 'wo': jax.random.normal(ks[5], (H, dh, W), jnp.float32) * s(H * dh), 'bo': jnp.zeros((W,), jnp.float32), 'proj_w': jax.random.normal(ks[6], (W, Dm), jnp.float32) * s(W), 'proj_b': jnp.zeros((Dm,), jnp.float32)}
    _L0_attn_in = _L0_attn_setup()

    def _L0_ffn_setup():
        import jax, jax.numpy as jnp
        import numpy as np
        MAX_THRESHOLD = 1.0 / 8.0
        SCALING = 32.0 / 16.0
        key = jax.random.key(seed)
        ks = jax.random.split(key, 8)
        B_, S, D, O, E, R = (4, 512, 1024, 1024, 8, 16)
        sd = 1.0 / np.sqrt(D)
        return {'x': jax.random.normal(ks[0], (B_, S, D), jnp.float32), 'W_base': jax.random.normal(ks[1], (O, D), jnp.float32) * sd, 'b_base': jax.random.normal(ks[2], (O,), jnp.float32) * 0.01, 'W_gate': jax.random.normal(ks[3], (E, D), jnp.float32) * sd, 'W_thr': jax.random.normal(ks[4], (1, D), jnp.float32) * sd, 'b_thr': jax.random.normal(ks[5], (1,), jnp.float32) * 0.01, 'A': jax.random.normal(ks[6], (E, R, D), jnp.float32) * sd, 'B': jax.random.normal(ks[7], (O,), jnp.float32)[None, :, None] * jnp.zeros((E, O, R), jnp.float32) + jax.random.normal(jax.random.fold_in(key, 7), (E, O, R), jnp.float32) * (1.0 / np.sqrt(R))}
    _L0_ffn_in = _L0_ffn_setup()
    _d = {'L0_attn_inputs': _L0_attn_in['inputs'], 'L0_attn_conv_w': _L0_attn_in['conv_w'], 'L0_attn_conv_b': _L0_attn_in['conv_b'], 'L0_attn_wq': _L0_attn_in['wq'], 'L0_attn_bq': _L0_attn_in['bq'], 'L0_attn_wk': _L0_attn_in['wk'], 'L0_attn_bk': _L0_attn_in['bk'], 'L0_attn_wv': _L0_attn_in['wv'], 'L0_attn_bv': _L0_attn_in['bv'], 'L0_attn_wo': _L0_attn_in['wo'], 'L0_attn_bo': _L0_attn_in['bo'], 'L0_attn_proj_w': _L0_attn_in['proj_w'], 'L0_attn_proj_b': _L0_attn_in['proj_b'], 'L0_ffn_W_base': _L0_ffn_in['W_base'], 'L0_ffn_b_base': _L0_ffn_in['b_base'], 'L0_ffn_W_gate': _L0_ffn_in['W_gate'], 'L0_ffn_W_thr': _L0_ffn_in['W_thr'], 'L0_ffn_b_thr': _L0_ffn_in['b_thr'], 'L0_ffn_A': _L0_ffn_in['A'], 'L0_ffn_B': _L0_ffn_in['B']}
    _x0 = _d['L0_attn_inputs']
    _d['L0_attn_inputs'] = jax.random.normal(jax.random.fold_in(jax.random.key(seed), 1), (2, 2048, 1024), dtype=_x0.dtype)
    del _x0
    return _d

def reference(L0_attn_inputs, L0_attn_conv_w, L0_attn_conv_b, L0_attn_wq, L0_attn_bq, L0_attn_wk, L0_attn_bk, L0_attn_wv, L0_attn_bv, L0_attn_wo, L0_attn_bo, L0_attn_proj_w, L0_attn_proj_b, L0_ffn_W_base, L0_ffn_b_base, L0_ffn_W_gate, L0_ffn_W_thr, L0_ffn_b_thr, L0_ffn_A, L0_ffn_B):

    def _L0_attn_ref(inputs, conv_w, conv_b, wq, bq, wk, bk, wv, bv, wo, bo, proj_w, proj_b):
        import jax, jax.numpy as jnp
        import numpy as np
        from jax import lax
        BLOCK_LEN = 128
        NEG_INF = -1000000000.0
        N, L, Dm = inputs.shape
        x = lax.conv_general_dilated(inputs, conv_w, window_strides=(1,), padding='SAME', dimension_numbers=('NWC', 'WIO', 'NWC')) + conv_b
        q, k, v = jnp.split(x, 3, axis=-1)
        W_ = q.shape[-1]
        nb = L // BLOCK_LEN
        q = q.reshape(N * nb, BLOCK_LEN, W_)
        k = k.reshape(N * nb, BLOCK_LEN, W_)
        v = v.reshape(N * nb, BLOCK_LEN, W_)
        dh = wq.shape[-1]
        qh = jnp.einsum('btd,dhe->bthe', q, wq) + bq
        kh = jnp.einsum('btd,dhe->bthe', k, wk) + bk
        vh = jnp.einsum('btd,dhe->bthe', v, wv) + bv
        scale = 1.0 / jnp.sqrt(jnp.asarray(dh, qh.dtype))
        scores = jnp.einsum('bqhe,bkhe->bhqk', qh * scale, kh)
        causal = jnp.tril(jnp.ones((BLOCK_LEN, BLOCK_LEN), bool))
        scores = jnp.where(causal, scores, NEG_INF)
        p = jax.nn.softmax(scores, axis=-1)
        o = jnp.einsum('bhqk,bkhe->bqhe', p, vh)
        o = jnp.einsum('bqhe,hed->bqd', o, wo) + bo
        o = o.reshape(N, L, W_)
        return o @ proj_w + proj_b

    def _L0_ffn_ref(x, W_base, b_base, W_gate, W_thr, b_thr, A, B):
        import jax, jax.numpy as jnp
        import numpy as np
        MAX_THRESHOLD = 1.0 / 8.0
        SCALING = 32.0 / 16.0
        base = jnp.einsum('bsd,od->bso', x, W_base) + b_base
        D = x.shape[-1]
        xf = x.reshape(-1, D)
        gate_logits = jax.nn.softmax(xf @ W_gate.T, axis=-1)
        thresholds = jax.nn.sigmoid(xf @ W_thr.T + b_thr) * MAX_THRESHOLD
        adapted = gate_logits - thresholds
        selected = (adapted >= 0).astype(x.dtype)
        weights = adapted * selected
        wsum = jnp.sum(weights, axis=-1, keepdims=True)
        wsum = jnp.where(wsum == 0, jnp.ones_like(wsum), wsum)
        weights = weights / wsum
        h = jnp.einsum('nd,erd->ner', xf, A)
        moe = jnp.einsum('ner,ne,eor->no', h, weights, B) * SCALING
        out = base + moe.reshape(base.shape)
        return out
    x = L0_attn_inputs
    x = _layernorm(x + _L0_attn_ref(x, L0_attn_conv_w, L0_attn_conv_b, L0_attn_wq, L0_attn_bq, L0_attn_wk, L0_attn_bk, L0_attn_wv, L0_attn_bv, L0_attn_wo, L0_attn_bo, L0_attn_proj_w, L0_attn_proj_b), axis=-1)
    x = _layernorm(x + _L0_ffn_ref(x, L0_ffn_W_base, L0_ffn_b_base, L0_ffn_W_gate, L0_ffn_W_thr, L0_ffn_b_thr, L0_ffn_A, L0_ffn_B), axis=-1)
    return x

_drawn_inputs = setup_inputs


def setup_inputs(seed=0):
    import zlib

    import numpy as np

    out = dict(_drawn_inputs(seed))
    spreads = {'L0_attn_conv_b': (0.0, 0.1),
     'L0_attn_bq': (0.0, 0.1),
     'L0_attn_bk': (0.0, 0.8),
     'L0_attn_bv': (0.0, 0.1),
     'L0_attn_bo': (0.0, 0.1),
     'L0_attn_proj_b': (0.0, 0.1)}
    factors = {'L0_ffn_b_base': 8.0}
    for name, (base, spread) in spreads.items():
        noise = np.random.default_rng([zlib.crc32(name.encode()), seed]).standard_normal(out[name].shape)
        drawn = base * np.exp(spread * noise) if base else spread * noise
        out[name] = jnp.asarray(drawn.astype(out[name].dtype))
    for name, factor in factors.items():
        out[name] = (out[name] * factor).astype(out[name].dtype)
    return out
```

```python
from contextlib import ExitStack

import numpy as np
import concourse.bass as bass
from concourse import mybir

F32 = mybir.dt.float32
F32R = mybir.dt.float32r
ALU = mybir.AluOpType
ACT = mybir.ActivationFunctionType
AX_X = mybir.AxisListType.X

P = 128
BATCH, SEQ, DM = 2, 2048, 1024
TOK = BATCH * SEQ
TAPS = 3
WB = 256
HEADS, DH = 16, 64
HE = HEADS * DH
EXPERTS, RANK = 8, 16
ER = EXPERTS * RANK
ST = 512
NST = TOK // ST
ST_SEQ = SEQ // ST
BLK = ST // P
NBLK = TOK // P
CC = DM // P
CF = 3 * WB // P
KC = WB // P
HP = HEADS // 2
WIN = ST + TAPS - 1
XS = 4
WCOLS = DM + ER + EXPERTS + 2
GATE0 = DM + ER
BANKS = ((0, 512), (512, 896), (896, WCOLS))
LAST = BANKS[2][1] - BANKS[2][0]
EPS = 1e-5
SCORE_SCALE = 1.0 / 8.0
MASKED = -1e30
LOWEST = -3.0e38
MAX_THRESHOLD, SCALING = 1.0 / 8.0, 2.0

HI, LO = 0, 1
PASSES = ((HI, HI), (HI, LO), (LO, HI))


def conv_phase(nc, xT, conv_w, conv_b, convT):
    with ExitStack() as ctx:
        def sb(name, shape, dt):
            return ctx.enter_context(nc.sbuf_tensor(name, shape, dt))

        def sem(name):
            return ctx.enter_context(nc.semaphore(name))

        w = sb("conv_weights", [P, CC, 2, TAPS, CF * P], F32R)
        wraw = sb("conv_w_raw", [P, 2, TAPS, CF * P], F32)
        xraw = sb("x_raw", [P, XS, WIN], F32)
        xs = sb("x_split", [P, XS, 2, WIN], F32R)
        out = sb("conv_out", [P, CF, ST], F32)
        bias = sb("conv_bias", [P, CF], F32)
        acc = [ctx.enter_context(nc.psum_tensor(f"conv_acc{f}", [P, ST], F32)) for f in range(CF)]

        bias_loaded = sem("conv_bias_loaded")
        w_loaded = [sem(f"conv_w_loaded{i}") for i in range(2)]
        x_loaded = [sem(f"x_loaded{i}") for i in range(XS)]
        w_hi, w_lo = sem("conv_w_hi"), sem("conv_w_lo")
        x_hi, x_lo = sem("x_hi"), sem("x_lo")
        x_used = sem("x_used")
        acc_done = sem("conv_acc_done")
        out_ready = sem("conv_out_ready")
        stored = sem("conv_stored")

        def wait_used(eng, t, c):
            if c >= XS:
                eng.wait_ge(x_used, (CC - 1) * t + c - XS + 1)
            elif not (isinstance(t, int) and t == 0):
                if c == XS - 1:
                    eng.wait_ge(acc_done, CF * t)
                else:
                    eng.wait_ge(x_used, (CC - 1) * (t - 1) + c + CC - XS + 1)

        block = ctx.enter_context(nc.Block())

        @block.sync
        def _(sp):
            sp.dma_start(bias[:], conv_b).then_inc(bias_loaded, 16)

            def load_x(t, c):
                if isinstance(t, int) and t == 0:
                    if c >= XS:
                        sp.wait_ge(x_lo, c - XS + 1)
                else:
                    sp.wait_ge(x_lo, CC * t + c - XS + 1)
                sp.dma_start(xraw[:, c % XS, :], xT[t, c]).then_inc(x_loaded[c % XS], 16)

            def store(t):
                sp.wait_ge(out_ready, CF * t + CF)
                sp.dma_start(convT[t], out[:]).then_inc(stored, 16)

            for c in range(CC):
                load_x(0, c)
                if c >= 2:
                    sp.wait_ge(w_lo, c - 1)
                sp.dma_start(wraw[:, c % 2, :, :], conv_w[c]).then_inc(w_loaded[c % 2], 16)
            with sp.Fori(1, NST) as t:
                for c in range(CC):
                    load_x(t, c)
                    if c == 3:
                        store(t - 1)
            store(NST - 1)
            sp.wait_ge(stored, 16 * NST)

        @block.scalar
        def _(act):
            def split_x(t, c):
                act.wait_ge(x_loaded[c % XS], 16 * (CC // XS * t + c // XS + 1))
                wait_used(act, t, c)
                nc.scalar.activation(xs[:, c % XS, HI, :], xraw[:, c % XS, :], ACT.Copy).then_inc(x_hi, 1)

            def evacuate(t):
                if not (isinstance(t, int) and t == 0):
                    act.wait_ge(stored, 16 * t)
                for f in range(CF):
                    act.wait_ge(acc_done, CF * t + f + 1)
                    nc.scalar.activation(out[:, f, :], acc[f][:], ACT.Identity,
                                         bias=bias[:, f:f + 1]).then_inc(out_ready, 1)

            for c in range(CC):
                split_x(0, c)
                act.wait_ge(w_loaded[c % 2], 16 * (c // 2 + 1))
                nc.scalar.activation(w[:, c, HI, :, :], wraw[:, c % 2, :, :], ACT.Copy).then_inc(w_hi, 1)
            act.wait_ge(bias_loaded, 16)
            with act.Fori(1, NST) as t:
                for c in range(CC):
                    split_x(t, c)
                    if c == 2:
                        evacuate(t - 1)
            evacuate(NST - 1)

        @block.vector
        def _(dve):
            def split_x(t, c):
                dve.wait_ge(x_hi, CC * t + c + 1)
                wait_used(dve, t, c)
                nc.vector.tensor_tensor(xs[:, c % XS, LO, :], xraw[:, c % XS, :],
                                        xs[:, c % XS, HI, :].bitcast(F32), ALU.subtract).then_inc(x_lo, 1)

            for c in range(CC):
                split_x(0, c)
                dve.wait_ge(w_hi, c + 1)
                nc.vector.tensor_tensor(w[:, c, LO, :, :], wraw[:, c % 2, :, :],
                                        w[:, c, HI, :, :].bitcast(F32), ALU.subtract).then_inc(w_lo, 1)
            with dve.Fori(1, NST) as t:
                for c in range(CC):
                    split_x(t, c)

        @block.tensor
        def _(pe):
            def chunk(t, c):
                first = isinstance(t, int) and t == 0
                if first:
                    pe.wait_ge(w_lo, c + 1)
                pe.wait_ge(x_lo, CC * t + c + 1)
                for f in range(CF):
                    if c == 0 and not first:
                        pe.wait_ge(out_ready, CF * (t - 1) + f + 1)
                    for k in range(TAPS):
                        for i, (a, b) in enumerate(PASSES):
                            last = nc.tensor.matmul(acc[f][:], w[:, c, a, k, f * P:(f + 1) * P],
                                                    xs[:, c % XS, b, k:k + ST],
                                                    start=(c == 0 and k == 0 and i == 0),
                                                    stop=(c == CC - 1 and k == TAPS - 1 and i == 2))
                    if c == CC - 1:
                        if f < CF - 1:
                            last.then_inc(acc_done, 1)
                last.then_inc(acc_done if c == CC - 1 else x_used, 1)

            def tile(t):
                for c in range(CC):
                    chunk(t, c)

            tile(0)
            with pe.Fori(1, NST) as t:
                tile(t)


def attention_phase(nc, convT, attn_w, q_bias, k_bias, v_bias, o_bias, yT):
    NW = KC * HE
    with ExitStack() as ctx:
        def sb(name, shape, dt):
            return ctx.enter_context(nc.sbuf_tensor(name, shape, dt))

        def psum(name):
            return ctx.enter_context(nc.psum_tensor(name, [P, ST], F32))

        def sem(name):
            return ctx.enter_context(nc.semaphore(name))

        w = sb("attn_weights", [P, 4, 2, NW], F32R)
        wraw = sb("attn_w_raw", [P, 2, NW], F32)
        craw = sb("conv_tile", [P, CF, ST], F32)
        cs = sb("conv_split", [P, 2, CF, ST], F32R)
        v = sb("v_heads", [P, BLK, HE], F32)
        qT = sb("q_pair", [P, 2, ST], F32)
        kT = sb("k_pair", [P, 2, ST], F32)
        scores = sb("scores", [P, 2, 2 * BLK, P], F32)
        probs = sb("probs", [P, 2, 2 * BLK, P], F32)
        probsT = sb("probs_T", [P, 2, ST], F32)
        top = sb("score_max", [P, 2, 2 * BLK], F32)
        ntop = sb("score_neg_max", [P, 2, 2 * BLK], F32)
        total = sb("prob_sum", [P, 2, 2 * BLK], F32)
        inv = sb("prob_inv_sum", [P, 2, 2 * BLK], F32)
        oT = sb("heads_out", [P, 2, HP, ST], F32R)
        y = sb("attn_out", [P, KC, ST], F32)
        mask = sb("causal_mask", [P, P], F32)
        ident = sb("identity", [P, P], F32)
        bq, bk = sb("q_bias", [P, HP], F32), sb("k_bias", [P, HP], F32)
        bv, bo = sb("v_bias_rows", [P, HE], F32), sb("o_bias", [P, KC], F32)
        ps_q, ps_k = psum("ps_q"), psum("ps_k")
        ps_s = [psum("ps_scores0"), psum("ps_scores1")]
        ps_t = [psum("ps_probsT0"), psum("ps_probsT1")]
        ps_o, ps_y = psum("ps_heads_out"), psum("ps_out")
        ps_v = [ps_q, ps_k]
        ps_m = [ps_y, ps_o]

        def wqkv(n, part, kc, cols):
            return w[:, n, part, :].rearrange("p (k n) -> p k n", k=KC)[:, kc, cols]

        def wo(part, s, cols):
            return w[:, 3, part, :].rearrange("p (k n) -> p k n", k=HP)[:, s, cols]

        bias_loaded = sem("attn_bias_loaded")
        w_loaded = [sem(f"attn_w_loaded{i}") for i in range(2)]
        w_hi, w_lo = sem("attn_w_hi"), sem("attn_w_lo")
        zeroed, masks = sem("attn_zeroed"), sem("attn_masks")
        c_loaded = sem("conv_tile_loaded")
        c_hi, c_lo = sem("conv_tile_hi"), sem("conv_tile_lo")
        v_done, v_ready = sem("v_done"), sem("v_ready")
        qk_done, q_ready, k_ready = sem("qk_done"), sem("q_ready"), sem("k_ready")
        scores_seen = sem("scores_seen")
        s_done = sem("scores_done")
        masked = sem("scores_masked")
        ntop_ready = sem("neg_max_ready")
        exps, inv_ready, normed = sem("exps"), sem("inv_sum_ready"), sem("probs_normed")
        t_done, t0_ready, t1_ready = sem("probsT_done"), sem("probsT0_ready"), sem("probsT1_ready")
        o_done, o_hi, o_lo = sem("heads_out_done"), sem("heads_out_hi"), sem("heads_out_lo")
        y_done, y_ready, stored = sem("attn_out_done"), sem("attn_out_ready"), sem("attn_out_stored")

        block = ctx.enter_context(nc.Block())
        VG = 2 * BLK

        @block.sync
        def _(sp):
            def load_conv(t, first):
                if not first:
                    sp.wait_ge(c_lo, 3 * t)
                sp.dma_start(craw[:], convT[t]).then_inc(c_loaded, 16)

            def store(t):
                sp.wait_ge(y_ready, KC * t + KC)
                sp.dma_start(yT[t], y[:]).then_inc(stored, 16)

            sp.dma_start(wraw[:, 0, :], attn_w[0]).then_inc(w_loaded[0], 16)
            load_conv(0, True)
            sp.dma_start(wraw[:, 1, :], attn_w[1]).then_inc(w_loaded[1], 16)
            for b, src in ((bq, q_bias), (bk, k_bias), (bv, v_bias.partition_broadcast(P)), (bo, o_bias)):
                sp.dma_start(b[:], src).then_inc(bias_loaded, 16)
            for n in (2, 3):
                sp.wait_ge(w_lo, n - 1)
                sp.dma_start(wraw[:, n % 2, :], attn_w[n]).then_inc(w_loaded[n % 2], 16)
            load_conv(1, False)
            with sp.Fori(1, NST - 1) as t:
                store(t - 1)
                load_conv(t + 1, False)
            store(NST - 2)
            store(NST - 1)
            sp.wait_ge(stored, 16 * NST)

        @block.gpsimd
        def _(pool):
            nc.gpsimd.memset(mask[:], 0.0).then_inc(zeroed, 1)
            nc.gpsimd.memset(ident[:], 0.0).then_inc(zeroed, 1)
            pool.wait_ge(zeroed, 2)
            nc.gpsimd.affine_select(out=mask[:], in_=mask[:], compare_op=ALU.is_ge, fill=MASKED, base=0,
                                    pattern=[[-1, P]], channel_multiplier=1).then_inc(masks, 1)
            nc.gpsimd.affine_select(out=ident[:], in_=ident[:], compare_op=ALU.not_equal, fill=1.0, base=0,
                                    pattern=[[-1, P]], channel_multiplier=1).then_inc(masks, 1)

        PARTS = ((4, 6), (0, 2), (2, 4))

        def pair(t, s):
            return HP * t + s

        @block.scalar
        def _(act):
            def split_conv(t, first):
                act.wait_ge(c_loaded, 16 * t + 16)
                if not first:
                    act.wait_ge(qk_done, 2 * HP * t)
                for a, b in PARTS:
                    nc.scalar.activation(cs[:, HI, a:b, :], craw[:, a:b, :], ACT.Copy).then_inc(c_hi, 1)

            def q_out(t, s):
                act.wait_ge(qk_done, 2 * pair(t, s) + 1)
                nc.scalar.activation(qT[:, s % 2, :], ps_q[:], ACT.Identity,
                                     bias=bq[:, s:s + 1]).then_inc(q_ready, 1)

            def exp(t, s):
                act.wait_ge(ntop_ready, pair(t, s) + 1)
                for i in range(2 * BLK):
                    last = nc.scalar.activation(probs[:, s % 2, i, :], scores[:, s % 2, i, :], ACT.Exp,
                                                bias=ntop[:, s % 2, i:i + 1], scale=SCORE_SCALE,
                                                accum_out=total[:, s % 2, i:i + 1])
                last.then_inc(exps, 1)

            def probsT_out(t, s):
                act.wait_ge(t_done, 2 * pair(t, s) + 1)
                nc.scalar.activation(probsT[:, 0, :], ps_t[0][:], ACT.Copy).then_inc(t0_ready, 1)

            def heads_out(t, s):
                act.wait_ge(o_done, pair(t, s) + 1)
                nc.scalar.activation(oT[:, HI, s, :], ps_o[:], ACT.Copy).then_inc(o_hi, 1)

            def out(t, first):
                if not first:
                    act.wait_ge(stored, 16 * t)
                for m in range(KC):
                    act.wait_ge(y_done, KC * t + m + 1)
                    nc.scalar.activation(y[:, m, :], ps_m[m][:], ACT.Identity,
                                         bias=bo[:, m:m + 1]).then_inc(y_ready, 1)

            def tile(t, first, last):
                for s in range(HP):
                    if s < HP - 1:
                        q_out(t, s + 1)
                    exp(t, s)
                    if s == 0 and not first:
                        out(t - 1, isinstance(t, int) and t == 1)
                    if s > 0:
                        heads_out(t, s - 1)
                    if s == HP - 1 and not last:
                        split_conv(t + 1, False)
                    probsT_out(t, s)
                if not last:
                    q_out(t + 1, 0)
                heads_out(t, HP - 1)

            act.wait_ge(w_loaded[0], 16)
            nc.scalar.activation(w[:, 0, HI, :], wraw[:, 0, :], ACT.Copy).then_inc(w_hi, 1)
            split_conv(0, True)
            for n in range(1, 4):
                act.wait_ge(w_loaded[n % 2], 16 * (n // 2 + 1))
                nc.scalar.activation(w[:, n, HI, :], wraw[:, n % 2, :], ACT.Copy).then_inc(w_hi, 1)
            act.wait_ge(bias_loaded, 64)
            q_out(0, 0)
            tile(0, True, False)
            tile(1, False, False)
            with act.Fori(2, NST - 1) as t:
                tile(t, False, False)
            tile(NST - 1, False, True)
            out(NST - 1, False)

        @block.vector
        def _(dve):
            def split_conv(t):
                for n, (a, b) in enumerate(PARTS):
                    dve.wait_ge(c_hi, 3 * t + n + 1)
                    nc.vector.tensor_tensor(cs[:, LO, a:b, :], craw[:, a:b, :], cs[:, HI, a:b, :].bitcast(F32),
                                            ALU.subtract).then_inc(c_lo, 1)

            def split_weights(n):
                dve.wait_ge(w_hi, n + 1)
                nc.vector.tensor_tensor(w[:, n, LO, :], wraw[:, n % 2, :], w[:, n, HI, :].bitcast(F32),
                                        ALU.subtract).then_inc(w_lo, 1)

            def v_out(t, h):
                for b in range(BLK):
                    dve.wait_ge(v_done, VG * t + BLK * h + b + 1)
                    nc.vector.tensor_tensor(v[:, b, h * ST:(h + 1) * ST], ps_v[b % 2][:],
                                            bv[:, h * ST:(h + 1) * ST], ALU.add).then_inc(v_ready, 1)

            def k_out(t, s):
                dve.wait_ge(qk_done, 2 * pair(t, s) + 2)
                nc.vector.tensor_scalar(kT[:, s % 2, :], ps_k[:], bk[:, s:s + 1], None, ALU.add).then_inc(k_ready, 1)

            def mask_max(t, s):
                for j in range(2):
                    dve.wait_ge(s_done, 2 * pair(t, s) + j + 1)
                    dve.sem_inc(scores_seen, 1)
                    for b in range(BLK):
                        i = j * BLK + b
                        last = nc.vector.tensor_tensor_reduce(
                            out=scores[:, s % 2, i, :], in0=ps_s[j][:, b * P:(b + 1) * P], in1=mask[:], scale=1.0,
                            scalar=LOWEST, op0=ALU.add, op1=ALU.max, accum_out=top[:, s % 2, i:i + 1])
                    last.then_inc(masked, 1)
                dve.wait_ge(masked, 2 * pair(t, s) + 2)
                nc.vector.tensor_scalar(ntop[:, s % 2, :], top[:, s % 2, :], -SCORE_SCALE, None,
                                        ALU.mult).then_inc(ntop_ready, 1)

            def normalize(t, s):
                dve.wait_ge(exps, pair(t, s) + 1)
                nc.vector.reciprocal(inv[:, s % 2, :], total[:, s % 2, :]).then_inc(inv_ready, 1)
                dve.wait_ge(inv_ready, pair(t, s) + 1)
                nc.vector.tensor_tensor(probs[:, s % 2, :, :], probs[:, s % 2, :, :],
                                        inv[:, s % 2, :].unsqueeze(2).broadcast_to([P, 2 * BLK, P]),
                                        ALU.mult).then_inc(normed, 1)

            def probsT_out(t, s):
                dve.wait_ge(t_done, 2 * pair(t, s) + 2)
                nc.vector.tensor_copy(probsT[:, 1, :], ps_t[1][:]).then_inc(t1_ready, 1)

            def heads_out(t, s):
                dve.wait_ge(o_hi, pair(t, s) + 1)
                nc.vector.tensor_tensor(oT[:, LO, s, :], ps_o[:], oT[:, HI, s, :].bitcast(F32),
                                        ALU.subtract).then_inc(o_lo, 1)

            def tile(t, last):
                for s in range(HP):
                    mask_max(t, s)
                    if s < HP - 1:
                        k_out(t, s + 1)
                    if s > 0:
                        heads_out(t, s - 1)
                    normalize(t, s)
                    if s == HP - 1 and not last:
                        split_conv(t + 1)
                        v_out(t + 1, 0)
                    probsT_out(t, s)
                if not last:
                    k_out(t + 1, 0)
                heads_out(t, HP - 1)
                if not last:
                    v_out(t + 1, 1)

            split_weights(0)
            split_conv(0)
            for n in range(1, 4):
                split_weights(n)
            dve.wait_ge(bias_loaded, 64)
            v_out(0, 0)
            k_out(0, 0)
            dve.wait_ge(masks, 2)
            v_out(0, 1)
            with dve.Fori(0, NST - 1) as t:
                tile(t, False)
            tile(NST - 1, True)

        @block.tensor
        def _(pe):
            def v_groups(t, h, first):
                if h == 0:
                    pe.wait_ge(c_lo, 3 * t + 1)
                for b in range(BLK):
                    if h == 0 and b < 2 and not first:
                        pe.wait_ge((q_ready, k_ready)[b], pair(t, 0))
                    elif h == 1 and b < 2:
                        pe.wait_ge((q_ready, k_ready)[b], pair(t, 0) + 1)
                    else:
                        if not (h == 0 and b < 2):
                            pe.wait_ge(v_ready, VG * t + BLK * h + b - 1)
                    n = 0
                    for kc in range(KC):
                        for a, c in PASSES:
                            last = nc.tensor.matmul(ps_v[b % 2][:], cs[:, a, 4 + kc, b * P:(b + 1) * P],
                                                    wqkv(2, c, kc, slice(h * ST, (h + 1) * ST)),
                                                    start=(n == 0), stop=(n == 5))
                            n += 1
                    last.then_inc(v_done, 1)

            def qk(t, s, first):
                if s == 0:
                    pe.wait_ge(c_lo, 3 * t + 3)
                    pe.wait_ge(v_ready, VG * t + BLK)
                elif s == 1:
                    pe.wait_ge(v_ready, VG * t + VG)
                for n, out in ((0, ps_q), (1, ps_k)):
                    if s >= 2:
                        pe.wait_ge((q_ready, k_ready)[n], pair(t, s))
                    i = 0
                    for kc in range(KC):
                        for a, c in PASSES:
                            last = nc.tensor.matmul(out[:], wqkv(n, a, kc, slice(s * P, (s + 1) * P)),
                                                    cs[:, c, 2 * n + kc, :], start=(i == 0), stop=(i == 5))
                            i += 1
                    last.then_inc(qk_done, 1)

            def qk_scores(t, s, first):
                pe.wait_ge(q_ready, pair(t, s) + 1)
                pe.wait_ge(k_ready, pair(t, s) + 1)
                if not first or s > 0:
                    pe.wait_ge(masked, 2 * pair(t, s))
                for j in range(2):
                    rows = slice(j * DH, (j + 1) * DH)
                    for b in range(BLK):
                        cols = slice(b * P, (b + 1) * P)
                        last = nc.tensor.matmul(ps_s[j][:, cols], qT[rows, s % 2, cols], kT[rows, s % 2, cols],
                                                start=True, stop=True)
                    last.then_inc(s_done, 1)

            def transposes(t, s, first):
                pe.wait_ge(normed, pair(t, s) + 1)
                if not first or s > 0:
                    pe.wait_ge(t0_ready, pair(t, s))
                    pe.wait_ge(t1_ready, pair(t, s))
                for j in range(2):
                    for b in range(BLK):
                        last = nc.tensor.transpose(ps_t[j][:, b * P:(b + 1) * P], probs[:, s % 2, j * BLK + b, :],
                                                   ident[:])
                    last.then_inc(t_done, 1)

            def weigh(t, s, first):
                pe.wait_ge(t0_ready, pair(t, s) + 1)
                pe.wait_ge(t1_ready, pair(t, s) + 1)
                if s > 0:
                    pe.wait_ge(o_lo, pair(t, s))
                elif not first:
                    pe.wait_ge(y_ready, KC * t)
                for j in range(2):
                    head = slice((2 * s + j) * DH, (2 * s + j + 1) * DH)
                    for b in range(BLK):
                        cols = slice(b * P, (b + 1) * P)
                        last = nc.tensor.matmul(ps_o[j * DH:(j + 1) * DH, cols], v[:, b, head], probsT[:, j, cols],
                                                start=True, stop=True)
                last.then_inc(o_done, 1)

            def out(t, first):
                pe.wait_ge(o_lo, pair(t, HP))
                if not first:
                    pe.wait_ge(y_ready, KC * t - 1)
                for m in range(KC):
                    i = 0
                    for s in range(HP):
                        for a, c in PASSES:
                            last = nc.tensor.matmul(ps_m[m][:], wo(a, s, slice(m * P, (m + 1) * P)), oT[:, c, s, :],
                                                    start=(i == 0), stop=(i == 3 * HP - 1))
                            i += 1
                    last.then_inc(y_done, 1)

            def tile(t, first, last):
                for s in range(HP):
                    qk_scores(t, s, first)
                    if s < HP - 1:
                        qk(t, s + 1, first)
                    if s == 0 and not first:
                        out(t - 1, isinstance(t, int) and t == 1)
                    if s > 0:
                        weigh(t, s - 1, first)
                    if s == HP - 1 and not last:
                        v_groups(t + 1, 0, False)
                    transposes(t, s, first)
                if not last:
                    qk(t + 1, 0, False)
                weigh(t, HP - 1, first)
                if not last:
                    v_groups(t + 1, 1, False)

            pe.wait_ge(w_lo, 3)
            v_groups(0, 0, True)
            qk(0, 0, True)
            pe.wait_ge(masks, 2)
            v_groups(0, 1, True)
            pe.wait_ge(w_lo, 4)
            tile(0, True, False)
            tile(1, False, False)
            with pe.Fori(2, NST - 1) as t:
                tile(t, False, False)
            tile(NST - 1, False, True)
            out(NST - 1, False)


def ffn_phase(nc, x, yT, proj_w, proj_b, ffn_w, lora_b, b_base, b_thr, out):
    with ExitStack() as ctx:
        def sb(name, shape, dt):
            return ctx.enter_context(nc.sbuf_tensor(name, shape, dt))

        def psum(name):
            return ctx.enter_context(nc.psum_tensor(name, [P, ST], F32))

        def sem(name):
            return ctx.enter_context(nc.semaphore(name))

        wp = sb("proj_weights", [P, KC, 2, DM], F32R)
        wf = sb("ffn_weights", [P, CC, 2, WCOLS], F32R)
        wb = sb("lora_b_weights", [P, 2, DM], F32R)
        wraw = sb("ffn_w_raw", [P, 2, WCOLS], F32)
        pb, bb = sb("proj_b_rows", [P, DM], F32), sb("base_b_rows", [P, DM], F32)
        bt = sb("thr_b", [P, 2], F32)
        ident = sb("identity2", [P, P], F32)
        xt = sb("x_tile", [P, 2, DM], F32)
        yr = sb("y_raw", [P, 2, KC, P], F32)
        ys = sb("y_split", [P, 2, 2, KC, P], F32R)
        x1 = sb("x1", [P, 2, DM], F32)
        x1b = sb("x1_plus_bias", [P, 2, DM], F32)
        x1T = sb("x1_T", [P, 2, CC, P], F32R)
        res = sb("residual_sum", [P, 2, DM], F32)
        ot = sb("out_tile", [P, 2, DM], F32)
        stats = sb("ln_stats", [P, 2, 2, 6], F32)
        mv = sb("ln_mean_var", [P, 2, 2], F32)
        var_eps, rstd = sb("ln_var_eps", [P, 2], F32), sb("ln_rstd", [P, 2], F32)
        minus_half, eps = sb("minus_half", [P, 1], F32), sb("eps", [P, 1], F32)
        hg = sb("h_and_gate", [P, LAST - P], F32)
        ngm = sb("gate_neg_max", [P, 1], F32)
        ge = sb("gate_exp", [P, EXPERTS], F32)
        den = sb("gate_denominators", [P, 2], F32)
        inv = sb("gate_inverses", [P, 2], F32)
        adapted = sb("gate_adapted", [P, EXPERTS], F32)
        wts = sb("gate_weights", [P, EXPERTS], F32)
        wsum = sb("gate_sum", [P, 3], F32)
        hw = sb("h_weighted", [P, ER], F32)
        hT = sb("h_weighted_T", [P, 2, P], F32R)
        ps_a = [psum("ps_a0"), psum("ps_a1")]
        ps_f = [[psum(f"ps_f{i}{n}") for n in range(3)] for i in range(2)]
        HT0 = LAST

        w_loaded = [sem(f"ffn_w_loaded{i}") for i in range(2)]
        w_hi, w_lo = sem("ffn_w_hi"), sem("ffn_w_lo")
        bias_loaded, bt_ready = sem("ffn_bias_loaded"), sem("thr_b_negated")
        id_zeroed, id_ready = sem("identity_zeroed"), sem("identity_ready")
        x_loaded = [sem(f"x_tile_loaded{i}") for i in range(2)]
        y_loaded = [sem(f"y_loaded{i}") for i in range(2)]
        xb_ready = sem("x_plus_bias_ready")
        y_hi, y_lo = sem("y_hi"), sem("y_lo")
        proj_done = sem("proj_done")
        res1_ready, res2_ready = sem("res1_ready"), sem("res2_ready")
        ln1_step, ln2_step = sem("ln1_step"), sem("ln2_step")
        var_ready = [sem(f"ln{k + 1}_var_ready") for k in range(2)]
        rstd_ready = [sem(f"ln{k + 1}_rstd_ready") for k in range(2)]
        stats_seen = sem("ln_stats_seen")
        x1_ready, x1b_ready = sem("x1_ready"), sem("x1b_ready")
        xT_done, xT_hi, xT_lo = sem("x1T_done"), sem("x1T_hi"), sem("x1T_lo")
        gate_done = sem("gate_done")
        base_done = sem("moe_done")
        hg_ready, ngm_ready, ge_ready = sem("h_gate_ready"), sem("gate_max_ready"), sem("gate_exp_ready")
        gate_step = sem("gate_step")
        hw_ready, hT_done = sem("h_weighted_ready"), sem("h_weighted_T_done")
        hT_hi, hT_lo = sem("h_weighted_T_hi"), sem("h_weighted_T_lo")
        out_ready = sem("out_ready")
        stored = [sem(f"out_stored{i}") for i in range(2)]

        block = ctx.enter_context(nc.Block())
        LN_STEPS, GATE_STEPS = 3, 7

        weights = [(proj_w[k], wp[:, k, :, :], DM) for k in range(KC)]
        weights += [(ffn_w[k], wf[:, k, :, :], WCOLS) for k in range(CC)]
        weights += [(lora_b, wb[:], DM)]
        NWT = len(weights)

        def windows(eng, window):
            for i in range(2):
                window(i, i, i)
            with eng.Fori(1, NBLK // 2 - 2) as m:
                for par in range(2):
                    window(2 * m + par, par, None)
            for i in range(NBLK - 4, NBLK):
                window(i, i % 2, i)

        def last(n, d):
            return n is not None and n + d >= NBLK

        @block.sync
        def _(sp):
            def load(i, par, reuse):
                if reuse:
                    sp.wait_ge(res1_ready, 2 * i - 2)
                sp.dma_start(xt[:, par, :], x[i]).then_inc(x_loaded[par], 16)
                if reuse:
                    sp.wait_ge(y_lo, i - 1)
                sp.dma_start(yr[:, par, :, :], yT[i]).then_inc(y_loaded[par], 16)

            def store(i, par):
                sp.wait_ge(out_ready, i + 1)
                sp.dma_start(out[i], ot[:, par, :]).then_inc(stored[par], 16)

            def window(i, par, n):
                if not last(n, 3):
                    load(i + 3, 1 - par, True)
                if n != 0:
                    store(i - 1, 1 - par)

            for n, (src, _, cols) in enumerate(weights):
                if n >= 2:
                    sp.wait_ge(w_lo, n - 1)
                sp.dma_start(wraw[:, n % 2, 0:cols], src).then_inc(w_loaded[n % 2], 16)
                if n < 2:
                    load(n, n, False)
                if n == 1:
                    for b, src in ((pb[:], proj_b), (bb[:], b_base), (bt[:, 0:1], b_thr)):
                        sp.dma_start(b, src.partition_broadcast(P)).then_inc(bias_loaded, 16)
            load(2, 0, True)
            windows(sp, window)
            store(NBLK - 1, 1)
            for par in range(2):
                sp.wait_ge(stored[par], 16 * (NBLK // 2))

        @block.gpsimd
        def _(pool):
            def add_proj_b(i, par):
                pool.wait_ge(x_loaded[par], 8 * (i - par) + 16)
                nc.gpsimd.tensor_tensor(xt[:, par, :], xt[:, par, :], pb[:], ALU.add).then_inc(xb_ready, 1)

            def add_base_b(i, par, reuse):
                pool.wait_ge(x1_ready, i + 1)
                if reuse:
                    pool.wait_ge(res2_ready, 3 * (i - 1))
                nc.gpsimd.tensor_tensor(x1b[:, par, :], x1[:, par, :], bb[:], ALU.add).then_inc(x1b_ready, 1)

            def inverse_root(i, k):
                pool.wait_ge((ln1_step, ln2_step)[k], 3 * i + 3)
                nc.gpsimd.tensor_tensor(var_eps[:, k:k + 1], mv[:, k, 1:2], eps[:], ALU.add).then_inc(var_ready[k], 1)
                pool.wait_ge(var_ready[k], i + 1)
                nc.gpsimd.tensor_tensor(rstd[:, k:k + 1], var_eps[:, k:k + 1], minus_half[:],
                                        ALU.pow).then_inc(rstd_ready[k], 1)

            def window(i, par, n):
                if not last(n, 1):
                    inverse_root(i + 1, 0)
                if not last(n, 2):
                    add_proj_b(i + 2, par)
                if n != 0:
                    inverse_root(i - 1, 1)
                if not last(n, 1):
                    add_base_b(i + 1, 1 - par, n != 0)

            nc.gpsimd.memset(ident[:], 0.0).then_inc(id_zeroed, 1)
            nc.gpsimd.memset(minus_half[:], -0.5).then_inc(id_zeroed, 1)
            nc.gpsimd.memset(eps[:], EPS).then_inc(id_zeroed, 1)
            pool.wait_ge(id_zeroed, 3)
            nc.gpsimd.affine_select(out=ident[:], in_=ident[:], compare_op=ALU.not_equal, fill=1.0, base=0,
                                    pattern=[[-1, P]], channel_multiplier=1).then_inc(id_ready, 1)
            pool.wait_ge(bias_loaded, 48)
            add_proj_b(0, 0)
            add_proj_b(1, 1)
            inverse_root(0, 0)
            add_base_b(0, 0, False)
            windows(pool, window)
            inverse_root(NBLK - 1, 1)

        @block.scalar
        def _(act):
            def split_y(i, par, reuse):
                act.wait_ge(y_loaded[par], 8 * (i - par) + 16)
                if reuse:
                    act.wait_ge(proj_done, 2 * (i - 1))
                nc.scalar.activation(ys[:, par, HI, :, :], yr[:, par, :, :], ACT.Copy).then_inc(y_hi, 1)

            def gate_exps(i):
                act.wait_ge(ngm_ready, i + 1)
                nc.scalar.activation(ge[:], hg[:, ER:ER + EXPERTS], ACT.Exp, bias=ngm[:, 0:1],
                                     accum_out=den[:, 0:1]).then_inc(ge_ready, 1)
                nc.scalar.activation(den[:, 1:2], hg[:, ER + EXPERTS:ER + EXPERTS + 1], ACT.Exp, scale=-1.0,
                                     bias=bt[:, 1:2]).then_inc(ge_ready, 1)

            def split_hT(i, par):
                act.wait_ge(hT_done, i + 1)
                nc.scalar.activation(hT[:, HI, :], ps_f[par][2][:, HT0:HT0 + P], ACT.Copy).then_inc(hT_hi, 1)

            def split_xT(i):
                for h in range(2):
                    act.wait_ge(xT_done, 2 * i + h + 1)
                    nc.scalar.activation(x1T[:, HI, 4 * h:4 * h + 4, :], ps_a[h][:], ACT.Copy).then_inc(xT_hi, 1)

            def window(i, par, n):
                if not last(n, 2):
                    split_y(i + 2, par, True)
                gate_exps(i)
                split_hT(i, par)
                if not last(n, 1):
                    split_xT(i + 1)

            for n, (_, w, cols) in enumerate(weights):
                act.wait_ge(w_loaded[n % 2], 16 * (n // 2 + 1))
                nc.scalar.activation(w[:, HI, :], wraw[:, n % 2, 0:cols], ACT.Copy,
                                     scale=SCALING if n == NWT - 1 else 1.0).then_inc(w_hi, 1)
                if n == 1:
                    split_y(0, 0, False)
                    split_y(1, 1, False)
            act.wait_ge(bias_loaded, 48)
            nc.scalar.mul(bt[:, 1:2], bt[:, 0:1], -1.0).then_inc(bt_ready, 1)
            act.wait_ge(bt_ready, 1)
            split_xT(0)
            windows(act, window)

        @block.vector
        def _(dve):
            def layernorm(i, k, src, dst, step, ready):
                base = LN_STEPS * i
                for h in range(2):
                    nc.vector.bn_stats(stats[:, k, h, :], src[:, h * ST:(h + 1) * ST]).then_inc(step, 1)
                dve.wait_ge(step, base + 2)
                dve.sem_inc(stats_seen, 1)
                nc.vector.bn_aggr(mv[:, k, :], stats[:, k, :, :]).then_inc(step, 1)
                dve.wait_ge(step, base + 3)
                dve.wait_ge(rstd_ready[k], i + 1)
                nc.vector.tensor_scalar(dst, src, mv[:, k, 0:1], rstd[:, k:k + 1], ALU.subtract,
                                        ALU.mult).then_inc(ready, 1)

            def first_norm(i, par, reuse):
                dve.wait_ge(xb_ready, i + 1)
                for h in range(2):
                    dve.wait_ge(proj_done, 2 * i + h + 1)
                    cols = slice(h * ST, (h + 1) * ST)
                    nc.vector.tensor_tensor(res[:, 0, cols], ps_a[h][:], xt[:, par, cols], ALU.add).then_inc(res1_ready, 1)
                dve.wait_ge(res1_ready, 2 * i + 2)
                if reuse:
                    dve.wait_ge(xT_done, 2 * i - 2)
                    dve.wait_ge(x1b_ready, i - 1)
                layernorm(i, 0, res[:, 0, :], x1[:, par, :], ln1_step, x1_ready)

            def second_norm(i, par, reuse):
                dve.wait_ge(x1b_ready, i + 1)
                dve.wait_ge(base_done, i + 1)
                for n, (a, b) in enumerate(BANKS):
                    b = min(b, DM)
                    nc.vector.tensor_tensor(res[:, 1, a:b], ps_f[par][n][:, 0:b - a], x1b[:, par, a:b],
                                            ALU.add).then_inc(res2_ready, 1)
                dve.wait_ge(res2_ready, 3 * i + 3)
                if reuse:
                    dve.wait_ge(stored[par], 8 * (i - par))
                layernorm(i, 1, res[:, 1, :], ot[:, par, :], ln2_step, out_ready)

            def split_y(i, par, reuse):
                dve.wait_ge(y_hi, i + 1)
                nc.vector.tensor_tensor(ys[:, par, LO, :, :], yr[:, par, :, :], ys[:, par, HI, :, :].bitcast(F32),
                                        ALU.subtract).then_inc(y_lo, 1)

            def gate(i, par):
                base = GATE_STEPS * i
                dve.wait_ge(gate_done, i + 1)
                nc.vector.tensor_copy(hg[:], ps_f[par][2][:, P:LAST]).then_inc(hg_ready, 1)
                dve.wait_ge(hg_ready, i + 1)
                nc.vector.tensor_reduce(ngm[:], hg[:, ER:ER + EXPERTS], AX_X, ALU.max, negate=True).then_inc(ngm_ready, 1)
                dve.wait_ge(ge_ready, 2 * i + 2)
                nc.vector.tensor_scalar(den[:, 1:2], den[:, 1:2], 1.0, 1.0 / MAX_THRESHOLD, ALU.add,
                                        ALU.mult).then_inc(gate_step, 1)
                dve.wait_ge(gate_step, base + 1)
                nc.vector.reciprocal(inv[:], den[:]).then_inc(gate_step, 1)
                dve.wait_ge(gate_step, base + 2)
                nc.vector.tensor_scalar(adapted[:], ge[:], inv[:, 0:1], inv[:, 1:2], ALU.mult,
                                        ALU.subtract).then_inc(gate_step, 1)
                dve.wait_ge(gate_step, base + 3)
                nc.vector.tensor_scalar(wts[:], adapted[:], 0.0, None, ALU.max).then_inc(gate_step, 1)
                dve.wait_ge(gate_step, base + 4)
                nc.vector.tensor_reduce(wsum[:, 0:1], wts[:], AX_X, ALU.add).then_inc(gate_step, 1)
                dve.wait_ge(gate_step, base + 5)
                nc.vector.scalar_tensor_tensor(out=wsum[:, 1:2], in0=wsum[:, 0:1], scalar=0.0, in1=wsum[:, 0:1],
                                               op0=ALU.is_equal, op1=ALU.add).then_inc(gate_step, 1)
                dve.wait_ge(gate_step, base + 6)
                nc.vector.reciprocal(wsum[:, 2:3], wsum[:, 1:2]).then_inc(gate_step, 1)
                dve.wait_ge(gate_step, base + 7)
                nc.vector.scalar_tensor_tensor(
                    out=hw[:].rearrange("p (e r) -> p e r", e=EXPERTS),
                    in0=hg[:, 0:ER].rearrange("p (e r) -> p e r", e=EXPERTS), scalar=wsum[:, 2:3],
                    in1=wts[:].unsqueeze(2).broadcast_to([P, EXPERTS, RANK]),
                    op0=ALU.mult, op1=ALU.mult).then_inc(hw_ready, 1)

            def split_hT(i, par):
                dve.wait_ge(hT_hi, i + 1)
                nc.vector.tensor_tensor(hT[:, LO, :], ps_f[par][2][:, HT0:HT0 + P], hT[:, HI, :].bitcast(F32),
                                        ALU.subtract).then_inc(hT_lo, 1)

            def split_xT(i):
                for h in range(2):
                    dve.wait_ge(xT_hi, 2 * i + h + 1)
                    part = slice(4 * h, 4 * h + 4)
                    nc.vector.tensor_tensor(x1T[:, LO, part, :], ps_a[h][:].rearrange("p (c n) -> p c n", c=4),
                                            x1T[:, HI, part, :].bitcast(F32), ALU.subtract).then_inc(xT_lo, 1)

            def window(i, par, n):
                if not last(n, 1):
                    first_norm(i + 1, 1 - par, n != 0)
                if not last(n, 2):
                    split_y(i + 2, par, True)
                gate(i, par)
                if n != 0:
                    second_norm(i - 1, 1 - par, n is None or n >= 3)
                split_hT(i, par)
                if not last(n, 1):
                    split_xT(i + 1)

            for n, (_, w, cols) in enumerate(weights):
                dve.wait_ge(w_hi, n + 1)
                raw, hi, lo = wraw[:, n % 2, 0:cols], w[:, HI, :].bitcast(F32), w[:, LO, :]
                if n < NWT - 1:
                    nc.vector.tensor_tensor(lo, raw, hi, ALU.subtract).then_inc(w_lo, 1)
                else:
                    nc.vector.scalar_tensor_tensor(out=lo, in0=raw, scalar=SCALING, in1=hi, op0=ALU.mult,
                                                   op1=ALU.subtract).then_inc(w_lo, 1)
                if n == 1:
                    split_y(0, 0, False)
                    split_y(1, 1, False)
            first_norm(0, 0, False)
            split_xT(0)
            windows(dve, window)
            second_norm(NBLK - 1, 1, True)

        @block.tensor
        def _(pe):
            def project(i, par, first):
                pe.wait_ge(y_lo, i + 1)
                if not first:
                    pe.wait_ge(xT_lo, 2 * i)
                for h in range(2):
                    n = 0
                    for kc in range(KC):
                        for a, b in PASSES:
                            mm = nc.tensor.matmul(ps_a[h][:], ys[:, par, a, kc, :], wp[:, kc, b, h * ST:(h + 1) * ST],
                                                  start=(n == 0), stop=(n == 5))
                            n += 1
                    mm.then_inc(proj_done, 1)

            def transpose_x1(i, par):
                pe.wait_ge(x1_ready, i + 1)
                for h in range(2):
                    for c in range(4):
                        mm = nc.tensor.transpose(ps_a[h][:, c * P:(c + 1) * P],
                                                 x1[:, par, (4 * h + c) * P:(4 * h + c + 1) * P], ident[:])
                    mm.then_inc(xT_done, 1)

            def base(i, par, reuse):
                pe.wait_ge(xT_lo, 2 * i + 2)
                if reuse:
                    pe.wait_ge(res2_ready, 3 * (i - 1))
                for n in (2, 0, 1):
                    a0, b0 = BANKS[n]
                    for kc in range(CC):
                        for k, (a, b) in enumerate(PASSES):
                            mm = nc.tensor.matmul(ps_f[par][n][:, 0:b0 - a0], x1T[:, a, kc, :], wf[:, kc, b, a0:b0],
                                                  start=(kc == 0 and k == 0), stop=(n == 2 and kc == CC - 1 and k == 2),
                                                  skip_group_check=True)
                    if n == 2:
                        mm.then_inc(gate_done, 1)

            def transpose_h(i, par):
                pe.wait_ge(hw_ready, i + 1)
                nc.tensor.matmul(ps_f[par][2][:, HT0:HT0 + P], hw[:], ident[:], is_transpose=True, start=False,
                                 stop=True, skip_group_check=True).then_inc(hT_done, 1)

            def experts(i, par):
                pe.wait_ge(hT_lo, i + 1)
                for n, (a0, b0) in enumerate(BANKS):
                    b0 = min(b0, DM)
                    for k, (a, b) in enumerate(PASSES):
                        mm = nc.tensor.matmul(ps_f[par][n][:, 0:b0 - a0], hT[:, a, :], wb[:, b, a0:b0],
                                              start=False, stop=(k == 2), skip_group_check=True)
                mm.then_inc(base_done, 1)

            def window(i, par, n):
                base(i, par, n is None or n >= 2)
                transpose_h(i, par)
                if not last(n, 1):
                    transpose_x1(i + 1, 1 - par)
                experts(i, par)
                if not last(n, 2):
                    project(i + 2, par, False)

            pe.wait_ge(w_lo, KC)
            project(0, 0, True)
            pe.wait_ge(id_ready, 1)
            transpose_x1(0, 0)
            project(1, 1, False)
            pe.wait_ge(w_lo, NWT)
            windows(pe, window)


def build(nc, ins, out):
    convT = nc.dram_tensor("convT_scratch", [NST, P, CF, ST], F32).ap()
    yT = nc.dram_tensor("yT_scratch", [P, KC, TOK], F32).ap()
    conv_phase(nc, ins["xT"], ins["conv_w"], ins["conv_b"], convT)
    attention_phase(nc, convT, ins["attn_w"], ins["q_bias"], ins["k_bias"], ins["v_bias"], ins["o_bias"],
                    TileColumns(yT, ST))
    ffn_phase(nc, ins["x"], TileColumns(yT, P), ins["proj_w"], ins["proj_b"], ins["ffn_w"], ins["lora_b"],
              ins["b_base"], ins["b_thr"], out)


class TileColumns:

    def __init__(self, ap, width):
        self.ap, self.width = ap, width

    def __getitem__(self, t):
        return self.ap[:, :, bass.ds(t * self.width, self.width)]


def kernel(**inputs):
    import concourse.bacc as bacc
    from concourse.bass_utils import run_bass_kernel_spmd

    a = {k: np.asarray(v) for k, v in inputs.items()}
    x = a["L0_attn_inputs"]
    padded = np.zeros((BATCH, DM, SEQ + TAPS - 1), x.dtype)
    padded[:, :, 1:SEQ + 1] = x.transpose(0, 2, 1)
    xT = np.stack([padded[t // ST_SEQ, :, (t % ST_SEQ) * ST:(t % ST_SEQ) * ST + WIN] for t in range(NST)])

    def chunks(w):
        return w.reshape(-1, P, w.shape[-1]).transpose(1, 0, 2)

    def columns(b):
        return b.reshape(-1, P).T

    w_in = [chunks(a[f"L0_attn_w{n}"].reshape(WB, HE)) for n in "qkv"]
    attn_w = np.stack([w.reshape(P, -1) for w in w_in + [chunks(a["L0_attn_wo"].reshape(HE, WB))]])
    ffn_w = np.concatenate([a["L0_ffn_W_base"], a["L0_ffn_A"].reshape(ER, DM), a["L0_ffn_W_gate"],
                            a["L0_ffn_W_thr"], np.zeros((1, DM), x.dtype)]).T
    arrays = {
        "xT": xT.reshape(NST, CC, P, WIN),
        "conv_w": a["L0_attn_conv_w"].reshape(TAPS, CC, P, 3 * WB).transpose(1, 2, 0, 3),
        "conv_b": columns(a["L0_attn_conv_b"]),
        "attn_w": attn_w,
        "q_bias": columns(a["L0_attn_bq"]),
        "k_bias": columns(a["L0_attn_bk"]),
        "v_bias": a["L0_attn_bv"].reshape(HE),
        "o_bias": columns(a["L0_attn_bo"]),
        "x": x.reshape(NBLK, P, DM),
        "proj_w": a["L0_attn_proj_w"].reshape(KC, P, DM),
        "proj_b": a["L0_attn_proj_b"],
        "ffn_w": ffn_w.reshape(CC, P, WCOLS),
        "lora_b": a["L0_ffn_B"].transpose(0, 2, 1).reshape(ER, DM),
        "b_base": a["L0_ffn_b_base"],
        "b_thr": a["L0_ffn_b_thr"],
    }
    arrays = {k: np.ascontiguousarray(v) for k, v in arrays.items()}
    nc = bacc.Bacc("TRN2", target_bir_lowering=False, num_devices=1)
    ins = {k: nc.dram_tensor(f"in_{k}", v.shape, mybir.dt.from_np(v.dtype), kind="ExternalInput").ap() for k, v in arrays.items()}
    out = nc.dram_tensor("out", [NBLK, P, DM], F32, kind="ExternalOutput").ap()
    build(nc, ins, out)
    result = run_bass_kernel_spmd(nc, [{f"in_{k}": v for k, v in arrays.items()}], core_ids=[0])
    return result.results[0]["out"].reshape(BATCH, SEQ, DM)
```

```python
from contextlib import ExitStack

import numpy as np
import concourse.bass as bass
from concourse import mybir

F32 = mybir.dt.float32
F32R = mybir.dt.float32r
ALU = mybir.AluOpType
ACT = mybir.ActivationFunctionType
AX_X = mybir.AxisListType.X

P = 128
BATCH, SEQ, DM = 2, 2048, 1024
TOK = BATCH * SEQ
TAPS = 3
WB = 256
HEADS, DH = 16, 64
HE = HEADS * DH
EXPERTS, RANK = 8, 16
ER = EXPERTS * RANK
ST = 512
NST = TOK // ST
ST_SEQ = SEQ // ST
BLK = ST // P
NBLK = TOK // P
CC = DM // P
CF = 3 * WB // P
KC = WB // P
HP = HEADS // 2
WIN = ST + TAPS - 1
XS = 4
WCOLS = DM + ER + EXPERTS + 2
GATE0 = DM + ER
BANKS = ((0, 512), (512, 896), (896, WCOLS))
LAST = BANKS[2][1] - BANKS[2][0]
EPS = 1e-5
SCORE_SCALE = 1.0 / 8.0
MASKED = -1e30
LOWEST = -3.0e38
MAX_THRESHOLD, SCALING = 1.0 / 8.0, 2.0

HI, LO = 0, 1
PASSES = ((HI, HI), (HI, LO), (LO, HI))


def conv_phase(nc, xT, conv_w, conv_b, convT):
    with ExitStack() as ctx:
        def sb(name, shape, dt):
            return ctx.enter_context(nc.sbuf_tensor(name, shape, dt))

        def sem(name):
            return ctx.enter_context(nc.semaphore(name))

        w = sb("conv_weights", [P, CC, 2, TAPS, CF * P], F32R)
        wraw = sb("conv_w_raw", [P, 2, TAPS, CF * P], F32)
        xraw = sb("x_raw", [P, XS, WIN], F32)
        xs = sb("x_split", [P, XS, 2, WIN], F32R)
        out = sb("conv_out", [P, CF, ST], F32)
        bias = sb("conv_bias", [P, CF], F32)
        acc = [ctx.enter_context(nc.psum_tensor(f"conv_acc{f}", [P, ST], F32)) for f in range(CF)]

        bias_loaded = sem("conv_bias_loaded")
        w_loaded = [sem(f"conv_w_loaded{i}") for i in range(2)]
        x_loaded = [sem(f"x_loaded{i}") for i in range(XS)]
        w_hi, w_lo = sem("conv_w_hi"), sem("conv_w_lo")
        x_hi, x_lo = sem("x_hi"), sem("x_lo")
        x_used = sem("x_used")
        acc_done = sem("conv_acc_done")
        out_ready = sem("conv_out_ready")
        stored = sem("conv_stored")

        def wait_used(eng, t, c):
            if c >= XS:
                eng.wait_ge(x_used, (CC - 1) * t + c - XS + 1)
            elif not (isinstance(t, int) and t == 0):
                if c == XS - 1:
                    eng.wait_ge(acc_done, CF * t)
                else:
                    eng.wait_ge(x_used, (CC - 1) * (t - 1) + c + CC - XS + 1)

        block = ctx.enter_context(nc.Block())

        @block.sync
        def _(sp):
            sp.dma_start(bias[:], conv_b).then_inc(bias_loaded, 16)

            def load_x(t, c):
                if isinstance(t, int) and t == 0:
                    if c >= XS:
                        sp.wait_ge(x_lo, c - XS + 1)
                else:
                    sp.wait_ge(x_lo, CC * t + c - XS + 1)
                sp.dma_start(xraw[:, c % XS, :], xT[t, c]).then_inc(x_loaded[c % XS], 16)

            def store(t):
                sp.wait_ge(out_ready, CF * t + CF)
                sp.dma_start(convT[t], out[:]).then_inc(stored, 16)

            for c in range(CC):
                load_x(0, c)
                if c >= 2:
                    sp.wait_ge(w_lo, c - 1)
                sp.dma_start(wraw[:, c % 2, :, :], conv_w[c]).then_inc(w_loaded[c % 2], 16)
            with sp.Fori(1, NST) as t:
                for c in range(CC):
                    load_x(t, c)
                    if c == 3:
                        store(t - 1)
            store(NST - 1)
            sp.wait_ge(stored, 16 * NST)

        @block.scalar
        def _(act):
            def split_x(t, c):
                act.wait_ge(x_loaded[c % XS], 16 * (CC // XS * t + c // XS + 1))
                wait_used(act, t, c)
                nc.scalar.activation(xs[:, c % XS, HI, :], xraw[:, c % XS, :], ACT.Copy).then_inc(x_hi, 1)

            def evacuate(t):
                if not (isinstance(t, int) and t == 0):
                    act.wait_ge(stored, 16 * t)
                for f in range(CF):
                    act.wait_ge(acc_done, CF * t + f + 1)
                    nc.scalar.activation(out[:, f, :], acc[f][:], ACT.Identity,
                                         bias=bias[:, f:f + 1]).then_inc(out_ready, 1)

            for c in range(CC):
                split_x(0, c)
                act.wait_ge(w_loaded[c % 2], 16 * (c // 2 + 1))
                nc.scalar.activation(w[:, c, HI, :, :], wraw[:, c % 2, :, :], ACT.Copy).then_inc(w_hi, 1)
            act.wait_ge(bias_loaded, 16)
            with act.Fori(1, NST) as t:
                for c in range(CC):
                    split_x(t, c)
                    if c == 2:
                        evacuate(t - 1)
            evacuate(NST - 1)

        @block.vector
        def _(dve):
            def split_x(t, c):
                dve.wait_ge(x_hi, CC * t + c + 1)
                wait_used(dve, t, c)
                nc.vector.tensor_tensor(xs[:, c % XS, LO, :], xraw[:, c % XS, :],
                                        xs[:, c % XS, HI, :].bitcast(F32), ALU.subtract).then_inc(x_lo, 1)

            for c in range(CC):
                split_x(0, c)
                dve.wait_ge(w_hi, c + 1)
                nc.vector.tensor_tensor(w[:, c, LO, :, :], wraw[:, c % 2, :, :],
                                        w[:, c, HI, :, :].bitcast(F32), ALU.subtract).then_inc(w_lo, 1)
            with dve.Fori(1, NST) as t:
                for c in range(CC):
                    split_x(t, c)

        @block.tensor
        def _(pe):
            def chunk(t, c):
                first = isinstance(t, int) and t == 0
                if first:
                    pe.wait_ge(w_lo, c + 1)
                pe.wait_ge(x_lo, CC * t + c + 1)
                for f in range(CF):
                    if c == 0 and not first:
                        pe.wait_ge(out_ready, CF * (t - 1) + f + 1)
                    for k in range(TAPS):
                        for i, (a, b) in enumerate(PASSES):
                            last = nc.tensor.matmul(acc[f][:], w[:, c, a, k, f * P:(f + 1) * P],
                                                    xs[:, c % XS, b, k:k + ST],
                                                    start=(c == 0 and k == 0 and i == 0),
                                                    stop=(c == CC - 1 and k == TAPS - 1 and i == 2))
                    if c == CC - 1:
                        if f < CF - 1:
                            last.then_inc(acc_done, 1)
                last.then_inc(acc_done if c == CC - 1 else x_used, 1)

            def tile(t):
                for c in range(CC):
                    chunk(t, c)

            tile(0)
            with pe.Fori(1, NST) as t:
                tile(t)


def attention_phase(nc, convT, attn_w, q_bias, k_bias, v_bias, o_bias, yT):
    NW = KC * HE
    PAIRS = NST * HP
    with ExitStack() as ctx:
        def sb(name, shape, dt):
            return ctx.enter_context(nc.sbuf_tensor(name, shape, dt))

        def psum(name):
            return ctx.enter_context(nc.psum_tensor(name, [P, ST], F32))

        def sem(name):
            return ctx.enter_context(nc.semaphore(name))

        w = sb("attn_weights", [P, 4, 2, NW], F32R)
        wraw = sb("attn_w_raw", [P, 2, NW], F32)
        craw = sb("conv_tile", [P, CF, ST], F32)
        cs = sb("conv_split", [P, 2, CF, ST], F32R)
        v = sb("v_heads", [P, BLK, HE], F32)
        qT = sb("q_pair", [P, 2, ST], F32)
        kT = sb("k_pair", [P, 2, ST], F32)
        scores = sb("scores", [P, 2, 2 * BLK, P], F32)
        probs = sb("probs", [P, 2, 2 * BLK, P], F32)
        top = sb("score_max", [P, 2, 2 * BLK], F32)
        ntop = sb("score_neg_max", [P, 2, 2 * BLK], F32)
        total = sb("prob_sum", [P, 2, 2 * BLK], F32)
        inv = sb("prob_inv_sum", [P, 2, 2 * BLK], F32)
        oT = sb("heads_out", [P, 2, 2, ST], F32R)
        probsT = sb("probs_T", [P, 2, ST], F32)
        y = sb("attn_out", [P, KC, ST], F32)
        mask = sb("causal_mask", [P, P], F32)
        ident = sb("identity", [P, P], F32)
        bq, bk = sb("q_bias", [P, HP], F32), sb("k_bias", [P, HP], F32)
        bv, bo = sb("v_bias_rows", [P, HE], F32), sb("o_bias", [P, KC], F32)
        ps_qt, ps_kt = psum("ps_q_and_probsT0"), psum("ps_k_and_probsT1")
        ps_s = [psum("ps_scores0"), psum("ps_scores1")]
        ps_o, ps_v = psum("ps_heads_out"), psum("ps_v")
        ps_y = [psum("ps_out0"), psum("ps_out1")]

        def wqkv(n, part, kc, cols):
            return w[:, n, part, :].rearrange("p (k n) -> p k n", k=KC)[:, kc, cols]

        def wo(part, s, cols):
            return w[:, 3, part, :].rearrange("p (k n) -> p k n", k=HP)[:, s, cols]

        bias_loaded = sem("attn_bias_loaded")
        w_loaded = [sem(f"attn_w_loaded{i}") for i in range(2)]
        w_hi, w_lo = sem("attn_w_hi"), sem("attn_w_lo")
        zeroed, masks = sem("attn_zeroed"), sem("attn_masks")
        c_loaded = sem("conv_tile_loaded")
        c_hi, c_lo = sem("conv_tile_hi"), sem("conv_tile_lo")
        v_done, v_ready = sem("v_done"), sem("v_ready")
        qk_done, q_ready, k_ready = sem("qk_done"), sem("q_ready"), sem("k_ready")
        s_done = sem("scores_done")
        scores_seen = sem("scores_seen")
        masked = sem("scores_masked")
        ntop_ready = sem("neg_max_ready")
        exps, inv_ready, normed = sem("exps"), sem("inv_sum_ready"), sem("probs_normed")
        t_done, t0_ready, t1_ready = sem("probsT_done"), sem("probsT0_ready"), sem("probsT1_ready")
        o_done, o_hi, o_lo = sem("heads_out_done"), sem("heads_out_hi"), sem("heads_out_lo")
        y_done, y_ready, stored = sem("attn_out_done"), sem("attn_out_ready"), sem("attn_out_stored")

        block = ctx.enter_context(nc.Block())
        V, Q, K = (4, 6), (0, 2), (2, 4)
        V_SPLIT, QK_SPLIT = 4, 5

        def pair(t, s):
            return HP * t + s

        def exists(t, s):
            return not isinstance(t, int) or 0 <= pair(t, s) < PAIRS

        def tiles(eng, tile):
            tile(0)
            with eng.Fori(1, NST - 1) as t:
                tile(t)
            tile(NST - 1)

        def v_group(t, s):
            return pair(t, s) + BLK, s % BLK, slice(ST, 2 * ST) if s < BLK else slice(0, ST)

        @block.sync
        def _(sp):
            def load_conv(t, first):
                if not first:
                    sp.wait_ge(c_lo, 3 * t)
                sp.dma_start(craw[:], convT[t]).then_inc(c_loaded, 16)

            def store(t):
                sp.wait_ge(y_ready, KC * t + KC)
                sp.dma_start(yT[t], y[:]).then_inc(stored, 16)

            sp.dma_start(wraw[:, 0, :], attn_w[0]).then_inc(w_loaded[0], 16)
            load_conv(0, True)
            sp.dma_start(wraw[:, 1, :], attn_w[1]).then_inc(w_loaded[1], 16)
            for b, src in ((bq, q_bias), (bk, k_bias), (bv, v_bias.partition_broadcast(P)), (bo, o_bias)):
                sp.dma_start(b[:], src).then_inc(bias_loaded, 16)
            for n in (2, 3):
                sp.wait_ge(w_lo, n - 1)
                sp.dma_start(wraw[:, n % 2, :], attn_w[n]).then_inc(w_loaded[n % 2], 16)
            load_conv(1, False)
            with sp.Fori(1, NST - 1) as t:
                store(t - 1)
                load_conv(t + 1, False)
            store(NST - 2)
            store(NST - 1)
            sp.wait_ge(stored, 16 * NST)

        @block.gpsimd
        def _(pool):
            nc.gpsimd.memset(mask[:], 0.0).then_inc(zeroed, 1)
            nc.gpsimd.memset(ident[:], 0.0).then_inc(zeroed, 1)
            pool.wait_ge(zeroed, 2)
            nc.gpsimd.affine_select(out=mask[:], in_=mask[:], compare_op=ALU.is_ge, fill=MASKED, base=0,
                                    pattern=[[-1, P]], channel_multiplier=1).then_inc(masks, 1)
            nc.gpsimd.affine_select(out=ident[:], in_=ident[:], compare_op=ALU.not_equal, fill=1.0, base=0,
                                    pattern=[[-1, P]], channel_multiplier=1).then_inc(masks, 1)

        @block.scalar
        def _(act):
            def split(parts):
                for a, b in parts:
                    nc.scalar.activation(cs[:, HI, a:b, :], craw[:, a:b, :], ACT.Copy).then_inc(c_hi, 1)

            def q_out(g, s):
                act.wait_ge(qk_done, 2 * g + 1)
                nc.scalar.activation(qT[:, s % 2, :], ps_qt[:], ACT.Identity, bias=bq[:, s:s + 1]).then_inc(q_ready, 1)

            def exp(g, s):
                for j in range(2):
                    act.wait_ge(ntop_ready, 2 * g + j + 1)
                    for i in range(j * BLK, (j + 1) * BLK):
                        last = nc.scalar.activation(probs[:, s % 2, i, :], scores[:, s % 2, i, :], ACT.Exp,
                                                    bias=ntop[:, s % 2, i:i + 1], scale=SCORE_SCALE,
                                                    accum_out=total[:, s % 2, i:i + 1])
                last.then_inc(exps, 1)

            def probsT_out(g):
                act.wait_ge(t_done, 2 * g + 1)
                nc.scalar.activation(probsT[:, 0, :], ps_qt[:], ACT.Copy).then_inc(t0_ready, 1)

            def heads_out(g, s):
                act.wait_ge(o_done, g + 1)
                nc.scalar.activation(oT[:, s % 2, HI, :], ps_o[:], ACT.Copy).then_inc(o_hi, 1)

            def out(t, first):
                if not first:
                    act.wait_ge(stored, 16 * t)
                for m in range(KC):
                    act.wait_ge(y_done, KC * t + m + 1)
                    nc.scalar.activation(y[:, m, :], ps_y[m][:], ACT.Identity, bias=bo[:, m:m + 1]).then_inc(y_ready, 1)

            def tile(t):
                for s in range(HP):
                    if s == V_SPLIT and exists(t, HP):
                        act.wait_ge(c_loaded, 16 * (t + 2))
                        act.wait_ge(v_done, pair(t, s) + BLK)
                        split([V])
                    if exists(t, s + 2):
                        q_out(pair(t, s + 2), (s + 2) % HP)
                    if s == QK_SPLIT and exists(t, HP):
                        act.wait_ge(qk_done, 2 * pair(t, HP))
                        split([Q, K])
                    if exists(t, s + 1):
                        exp(pair(t, s + 1), s + 1)
                    probsT_out(pair(t, s))
                    if exists(t, s - 1):
                        heads_out(pair(t, s - 1), s - 1)
                    if s == 2 and exists(t, -1):
                        out(t - 1, isinstance(t, int) and t == 1)

            act.wait_ge(w_loaded[0], 16)
            nc.scalar.activation(w[:, 0, HI, :], wraw[:, 0, :], ACT.Copy).then_inc(w_hi, 1)
            act.wait_ge(c_loaded, 16)
            split([V, Q, K])
            for n in range(1, 4):
                act.wait_ge(w_loaded[n % 2], 16 * (n // 2 + 1))
                nc.scalar.activation(w[:, n, HI, :], wraw[:, n % 2, :], ACT.Copy).then_inc(w_hi, 1)
            act.wait_ge(bias_loaded, 64)
            q_out(0, 0)
            q_out(1, 1)
            exp(0, 0)
            tiles(act, tile)
            heads_out(PAIRS - 1, HP - 1)
            out(NST - 1, False)

        @block.vector
        def _(dve):
            def split(t, parts):
                for n, (a, b) in parts:
                    dve.wait_ge(c_hi, 3 * t + n + 1)
                    nc.vector.tensor_tensor(cs[:, LO, a:b, :], craw[:, a:b, :], cs[:, HI, a:b, :].bitcast(F32),
                                            ALU.subtract).then_inc(c_lo, 1)

            def split_weights(n):
                dve.wait_ge(w_hi, n + 1)
                nc.vector.tensor_tensor(w[:, n, LO, :], wraw[:, n % 2, :], w[:, n, HI, :].bitcast(F32),
                                        ALU.subtract).then_inc(w_lo, 1)

            def v_out(n, b, cols):
                dve.wait_ge(v_done, n + 1)
                nc.vector.tensor_tensor(v[:, b, cols], ps_v[:], bv[:, cols], ALU.add).then_inc(v_ready, 1)

            def k_out(g, s):
                dve.wait_ge(qk_done, 2 * g + 2)
                nc.vector.tensor_scalar(kT[:, s % 2, :], ps_kt[:], bk[:, s:s + 1], None, ALU.add).then_inc(k_ready, 1)

            def mask_max(g, s):
                for j in range(2):
                    dve.wait_ge(s_done, 2 * g + j + 1)
                    dve.sem_inc(scores_seen, 1)
                    heads = slice(j * BLK, (j + 1) * BLK)
                    for b in range(BLK):
                        i = j * BLK + b
                        last = nc.vector.tensor_tensor_reduce(
                            out=scores[:, s % 2, i, :], in0=ps_s[j][:, b * P:(b + 1) * P], in1=mask[:], scale=1.0,
                            scalar=LOWEST, op0=ALU.add, op1=ALU.max, accum_out=top[:, s % 2, i:i + 1])
                    last.then_inc(masked, 1)
                    dve.wait_ge(masked, 2 * g + j + 1)
                    nc.vector.tensor_scalar(ntop[:, s % 2, heads], top[:, s % 2, heads], -SCORE_SCALE, None,
                                            ALU.mult).then_inc(ntop_ready, 1)

            def normalize(g, s):
                dve.wait_ge(exps, g + 1)
                nc.vector.reciprocal(inv[:, s % 2, :], total[:, s % 2, :]).then_inc(inv_ready, 1)
                dve.wait_ge(inv_ready, g + 1)
                nc.vector.tensor_tensor(probs[:, s % 2, :, :], probs[:, s % 2, :, :],
                                        inv[:, s % 2, :].unsqueeze(2).broadcast_to([P, 2 * BLK, P]),
                                        ALU.mult).then_inc(normed, 1)

            def probsT_out(g):
                dve.wait_ge(t_done, 2 * g + 2)
                nc.vector.tensor_copy(probsT[:, 1, :], ps_kt[:]).then_inc(t1_ready, 1)

            def heads_out(g, s):
                dve.wait_ge(o_hi, g + 1)
                nc.vector.tensor_tensor(oT[:, s % 2, LO, :], ps_o[:], oT[:, s % 2, HI, :].bitcast(F32),
                                        ALU.subtract).then_inc(o_lo, 1)

            def tile(t):
                for s in range(HP):
                    normalize(pair(t, s), s)
                    if s == V_SPLIT and exists(t, HP):
                        split(t + 1, [(0, V)])
                    if exists(t, s + 2):
                        k_out(pair(t, s + 2), (s + 2) % HP)
                    if s == QK_SPLIT and exists(t, HP):
                        split(t + 1, [(1, Q), (2, K)])
                    if exists(t, s + 1):
                        mask_max(pair(t, s + 1), s + 1)
                    probsT_out(pair(t, s))
                    if s < BLK or exists(t, HP):
                        v_out(*v_group(t, s))
                    if exists(t, s - 1):
                        heads_out(pair(t, s - 1), s - 1)

            split_weights(0)
            split(0, [(0, V), (1, Q), (2, K)])
            for n in range(1, 4):
                split_weights(n)
            dve.wait_ge(bias_loaded, 64)
            for b in range(BLK):
                v_out(b, b, slice(0, ST))
            k_out(0, 0)
            k_out(1, 1)
            dve.wait_ge(masks, 2)
            mask_max(0, 0)
            tiles(dve, tile)
            heads_out(PAIRS - 1, HP - 1)

        @block.tensor
        def _(pe):
            def project_v(n, b, cols):
                if not (isinstance(n, int) and n == 0):
                    pe.wait_ge(v_ready, n)
                i = 0
                for kc in range(KC):
                    for a, c in PASSES:
                        last = nc.tensor.matmul(ps_v[:], cs[:, a, V[0] + kc, b * P:(b + 1) * P], wqkv(2, c, kc, cols),
                                                start=(i == 0), stop=(i == 5))
                        i += 1
                last.then_inc(v_done, 1)

            def project_qk(g, s, copied=None, count=0):
                for n, out in ((0, ps_qt), (1, ps_kt)):
                    if copied is not None:
                        pe.wait_ge(copied[n], count)
                    i = 0
                    for kc in range(KC):
                        for a, c in PASSES:
                            last = nc.tensor.matmul(out[:], wqkv(n, a, kc, slice(s * P, (s + 1) * P)),
                                                    cs[:, c, 2 * n + kc, :], start=(i == 0), stop=(i == 5))
                            i += 1
                    last.then_inc(qk_done, 1)

            def make_scores(g, s, first):
                pe.wait_ge(q_ready, g + 1)
                pe.wait_ge(k_ready, g + 1)
                if not first:
                    pe.wait_ge(masked, 2 * g)
                for j in range(2):
                    rows = slice(j * DH, (j + 1) * DH)
                    for b in range(BLK):
                        cols = slice(b * P, (b + 1) * P)
                        last = nc.tensor.matmul(ps_s[j][:, cols], qT[rows, s % 2, cols], kT[rows, s % 2, cols],
                                                start=True, stop=True)
                    last.then_inc(s_done, 1)

            def transpose_probs(g, s, projected):
                pe.wait_ge(normed, g + 1)
                pe.wait_ge(q_ready, projected)
                pe.wait_ge(k_ready, projected)
                for j, out in enumerate((ps_qt, ps_kt)):
                    for b in range(BLK):
                        last = nc.tensor.transpose(out[:, b * P:(b + 1) * P], probs[:, s % 2, j * BLK + b, :], ident[:])
                    last.then_inc(t_done, 1)

            def weigh_v(g, s, groups, first):
                pe.wait_ge(t0_ready, g + 1)
                pe.wait_ge(t1_ready, g + 1)
                pe.wait_ge(v_ready, groups)
                if not first:
                    pe.wait_ge(o_lo, g)
                for j in range(2):
                    head = slice((2 * s + j) * DH, (2 * s + j + 1) * DH)
                    for b in range(BLK):
                        cols = slice(b * P, (b + 1) * P)
                        last = nc.tensor.matmul(ps_o[j * DH:(j + 1) * DH, cols], v[:, b, head], probsT[:, j, cols],
                                                start=True, stop=True)
                last.then_inc(o_done, 1)

            def add_out(t, g, s, first):
                pe.wait_ge(o_lo, g + 1)
                if s == 0 and not first:
                    pe.wait_ge(y_ready, KC * t)
                for m in range(KC):
                    for i, (a, c) in enumerate(PASSES):
                        last = nc.tensor.matmul(ps_y[m][:], wo(a, s, slice(m * P, (m + 1) * P)), oT[:, s % 2, c, :],
                                                start=(s == 0 and i == 0), stop=(s == HP - 1 and i == 2))
                    if s == HP - 1:
                        last.then_inc(y_done, 1)

            def tile(t):
                zero = isinstance(t, int) and t == 0
                for s in range(HP):
                    g = pair(t, s)
                    if exists(t, s + 2):
                        if s + 2 == HP:
                            pe.wait_ge(c_lo, 3 * (t + 1) + 3)
                        project_qk(g + 2, (s + 2) % HP, (q_ready, k_ready) if zero and s == 0 else (t0_ready, t1_ready),
                                   2 if zero and s == 0 else g)
                    if exists(t, s + 1):
                        make_scores(g + 1, s + 1, False)
                    if exists(t, s - 1):
                        weigh_v(g - 1, (s - 1) % HP, pair(t, BLK) if 1 <= s <= BLK else
                                pair(t, 2 * BLK) if s else pair(t, 0), zero and s == 1)
                    transpose_probs(g, s, g + 3 if exists(t, s + 2) else PAIRS)
                    if s < BLK or exists(t, HP):
                        if s == BLK:
                            pe.wait_ge(c_lo, 3 * (t + 1) + 1)
                        project_v(*v_group(t, s))
                    if exists(t, s - 2):
                        add_out(t if s >= 2 else t - 1, g - 2, (s - 2) % HP, zero)

            pe.wait_ge(w_lo, 3)
            pe.wait_ge(c_lo, 3)
            for b in range(BLK):
                project_v(b, b, slice(0, ST))
            project_qk(0, 0)
            project_qk(1, 1, (q_ready, k_ready), 1)
            make_scores(0, 0, True)
            pe.wait_ge(masks, 2)
            pe.wait_ge(w_lo, 4)
            tiles(pe, tile)
            weigh_v(PAIRS - 1, HP - 1, pair(NST, 0), False)
            for g in (PAIRS - 2, PAIRS - 1):
                add_out(NST - 1, g, g % HP, False)


def ffn_phase(nc, x, yT, proj_w, proj_b, ffn_w, lora_b, b_base, b_thr, out):
    with ExitStack() as ctx:
        def sb(name, shape, dt):
            return ctx.enter_context(nc.sbuf_tensor(name, shape, dt))

        def psum(name):
            return ctx.enter_context(nc.psum_tensor(name, [P, ST], F32))

        def sem(name):
            return ctx.enter_context(nc.semaphore(name))

        wp = sb("proj_weights", [P, KC, 2, DM], F32R)
        wf = sb("ffn_weights", [P, CC, 2, WCOLS], F32R)
        wb = sb("lora_b_weights", [P, 2, DM], F32R)
        wraw = sb("ffn_w_raw", [P, 2, WCOLS], F32)
        pb, bb = sb("proj_b_rows", [P, DM], F32), sb("base_b_rows", [P, DM], F32)
        bt = sb("thr_b", [P, 2], F32)
        ident = sb("identity2", [P, P], F32)
        xt = sb("x_tile", [P, 2, DM], F32)
        yr = sb("y_raw", [P, 2, KC, P], F32)
        ys = sb("y_split", [P, 2, 2, KC, P], F32R)
        x1 = sb("x1", [P, 2, DM], F32)
        x1b = sb("x1_plus_bias", [P, 2, DM], F32)
        x1T = sb("x1_T", [P, 2, CC, P], F32R)
        res = sb("residual_sum", [P, 2, DM], F32)
        ot = sb("out_tile", [P, 2, DM], F32)
        stats = sb("ln_stats", [P, 2, 2, 6], F32)
        mv = sb("ln_mean_var", [P, 2, 2], F32)
        var_eps, rstd = sb("ln_var_eps", [P, 2], F32), sb("ln_rstd", [P, 2], F32)
        minus_half, eps = sb("minus_half", [P, 1], F32), sb("eps", [P, 1], F32)
        hg = sb("h_and_gate", [P, LAST - P], F32)
        ngm = sb("gate_neg_max", [P, 1], F32)
        ge = sb("gate_exp", [P, EXPERTS], F32)
        den = sb("gate_denominators", [P, 2], F32)
        inv = sb("gate_inverses", [P, 2], F32)
        adapted = sb("gate_adapted", [P, EXPERTS], F32)
        wts = sb("gate_weights", [P, EXPERTS], F32)
        wsum = sb("gate_sum", [P, 3], F32)
        hw = sb("h_weighted", [P, ER], F32)
        hT = sb("h_weighted_T", [P, 2, P], F32R)
        ps_a = [psum("ps_a0"), psum("ps_a1")]
        ps_f = [[psum(f"ps_f{i}{n}") for n in range(3)] for i in range(2)]
        HT0 = LAST

        w_loaded = [sem(f"ffn_w_loaded{i}") for i in range(2)]
        w_hi, w_lo = sem("ffn_w_hi"), sem("ffn_w_lo")
        bias_loaded, bt_ready = sem("ffn_bias_loaded"), sem("thr_b_negated")
        id_zeroed, id_ready = sem("identity_zeroed"), sem("identity_ready")
        x_loaded = [sem(f"x_tile_loaded{i}") for i in range(2)]
        y_loaded = [sem(f"y_loaded{i}") for i in range(2)]
        xb_ready = sem("x_plus_bias_ready")
        y_hi, y_lo = sem("y_hi"), sem("y_lo")
        proj_done = sem("proj_done")
        res1_ready, res2_ready = sem("res1_ready"), sem("res2_ready")
        ln1_step, ln2_step = sem("ln1_step"), sem("ln2_step")
        var_ready = [sem(f"ln{k + 1}_var_ready") for k in range(2)]
        rstd_ready = [sem(f"ln{k + 1}_rstd_ready") for k in range(2)]
        stats_seen = sem("ln_stats_seen")
        x1_ready, x1b_ready = sem("x1_ready"), sem("x1b_ready")
        xT_done, xT_hi, xT_lo = sem("x1T_done"), sem("x1T_hi"), sem("x1T_lo")
        gate_done = sem("gate_done")
        base_done = sem("moe_done")
        hg_ready, ngm_ready, ge_ready = sem("h_gate_ready"), sem("gate_max_ready"), sem("gate_exp_ready")
        gate_step = sem("gate_step")
        hw_ready, hT_done = sem("h_weighted_ready"), sem("h_weighted_T_done")
        hT_hi, hT_lo = sem("h_weighted_T_hi"), sem("h_weighted_T_lo")
        out_ready = sem("out_ready")
        stored = [sem(f"out_stored{i}") for i in range(2)]

        block = ctx.enter_context(nc.Block())
        LN_STEPS, GATE_STEPS = 3, 7

        weights = [(proj_w[k], wp[:, k, :, :], DM) for k in range(KC)]
        weights += [(ffn_w[k], wf[:, k, :, :], WCOLS) for k in range(CC)]
        weights += [(lora_b, wb[:], DM)]
        NWT = len(weights)

        def windows(eng, window):
            for i in range(2):
                window(i, i, i)
            with eng.Fori(1, NBLK // 2 - 2) as m:
                for par in range(2):
                    window(2 * m + par, par, None)
            for i in range(NBLK - 4, NBLK):
                window(i, i % 2, i)

        def last(n, d):
            return n is not None and n + d >= NBLK

        @block.sync
        def _(sp):
            def load(i, par, reuse):
                if reuse:
                    sp.wait_ge(res1_ready, 2 * i - 2)
                sp.dma_start(xt[:, par, :], x[i]).then_inc(x_loaded[par], 16)
                if reuse:
                    sp.wait_ge(y_lo, i - 1)
                sp.dma_start(yr[:, par, :, :], yT[i]).then_inc(y_loaded[par], 16)

            def store(i, par):
                sp.wait_ge(out_ready, i + 1)
                sp.dma_start(out[i], ot[:, par, :]).then_inc(stored[par], 16)

            def window(i, par, n):
                if not last(n, 3):
                    load(i + 3, 1 - par, True)
                if n != 0:
                    store(i - 1, 1 - par)

            for n, (src, _, cols) in enumerate(weights):
                if n >= 2:
                    sp.wait_ge(w_lo, n - 1)
                sp.dma_start(wraw[:, n % 2, 0:cols], src).then_inc(w_loaded[n % 2], 16)
                if n < 2:
                    load(n, n, False)
                if n == 1:
                    for b, src in ((pb[:], proj_b), (bb[:], b_base), (bt[:, 0:1], b_thr)):
                        sp.dma_start(b, src.partition_broadcast(P)).then_inc(bias_loaded, 16)
            load(2, 0, True)
            windows(sp, window)
            store(NBLK - 1, 1)
            for par in range(2):
                sp.wait_ge(stored[par], 16 * (NBLK // 2))

        @block.gpsimd
        def _(pool):
            def add_proj_b(i, par):
                pool.wait_ge(x_loaded[par], 8 * (i - par) + 16)
                nc.gpsimd.tensor_tensor(xt[:, par, :], xt[:, par, :], pb[:], ALU.add).then_inc(xb_ready, 1)

            def add_base_b(i, par, reuse):
                pool.wait_ge(x1_ready, i + 1)
                if reuse:
                    pool.wait_ge(res2_ready, 3 * (i - 1))
                nc.gpsimd.tensor_tensor(x1b[:, par, :], x1[:, par, :], bb[:], ALU.add).then_inc(x1b_ready, 1)

            def inverse_root(i, k):
                pool.wait_ge((ln1_step, ln2_step)[k], 3 * i + 3)
                nc.gpsimd.tensor_tensor(var_eps[:, k:k + 1], mv[:, k, 1:2], eps[:], ALU.add).then_inc(var_ready[k], 1)
                pool.wait_ge(var_ready[k], i + 1)
                nc.gpsimd.tensor_tensor(rstd[:, k:k + 1], var_eps[:, k:k + 1], minus_half[:],
                                        ALU.pow).then_inc(rstd_ready[k], 1)

            def window(i, par, n):
                if not last(n, 1):
                    inverse_root(i + 1, 0)
                if not last(n, 2):
                    add_proj_b(i + 2, par)
                if n != 0:
                    inverse_root(i - 1, 1)
                if not last(n, 1):
                    add_base_b(i + 1, 1 - par, n != 0)

            nc.gpsimd.memset(ident[:], 0.0).then_inc(id_zeroed, 1)
            nc.gpsimd.memset(minus_half[:], -0.5).then_inc(id_zeroed, 1)
            nc.gpsimd.memset(eps[:], EPS).then_inc(id_zeroed, 1)
            pool.wait_ge(id_zeroed, 3)
            nc.gpsimd.affine_select(out=ident[:], in_=ident[:], compare_op=ALU.not_equal, fill=1.0, base=0,
                                    pattern=[[-1, P]], channel_multiplier=1).then_inc(id_ready, 1)
            pool.wait_ge(bias_loaded, 48)
            add_proj_b(0, 0)
            add_proj_b(1, 1)
            inverse_root(0, 0)
            add_base_b(0, 0, False)
            windows(pool, window)
            inverse_root(NBLK - 1, 1)

        @block.scalar
        def _(act):
            def split_y(i, par, reuse):
                act.wait_ge(y_loaded[par], 8 * (i - par) + 16)
                if reuse:
                    act.wait_ge(proj_done, 2 * (i - 1))
                nc.scalar.activation(ys[:, par, HI, :, :], yr[:, par, :, :], ACT.Copy).then_inc(y_hi, 1)

            def gate_exps(i):
                act.wait_ge(ngm_ready, i + 1)
                nc.scalar.activation(ge[:], hg[:, ER:ER + EXPERTS], ACT.Exp, bias=ngm[:, 0:1],
                                     accum_out=den[:, 0:1]).then_inc(ge_ready, 1)
                nc.scalar.activation(den[:, 1:2], hg[:, ER + EXPERTS:ER + EXPERTS + 1], ACT.Exp, scale=-1.0,
                                     bias=bt[:, 1:2]).then_inc(ge_ready, 1)

            def split_hT(i, par):
                act.wait_ge(hT_done, i + 1)
                nc.scalar.activation(hT[:, HI, :], ps_f[par][2][:, HT0:HT0 + P], ACT.Copy).then_inc(hT_hi, 1)

            def split_xT(i):
                for h in range(2):
                    act.wait_ge(xT_done, 2 * i + h + 1)
                    nc.scalar.activation(x1T[:, HI, 4 * h:4 * h + 4, :], ps_a[h][:], ACT.Copy).then_inc(xT_hi, 1)

            def window(i, par, n):
                if not last(n, 2):
                    split_y(i + 2, par, True)
                gate_exps(i)
                split_hT(i, par)
                if not last(n, 1):
                    split_xT(i + 1)

            for n, (_, w, cols) in enumerate(weights):
                act.wait_ge(w_loaded[n % 2], 16 * (n // 2 + 1))
                nc.scalar.activation(w[:, HI, :], wraw[:, n % 2, 0:cols], ACT.Copy,
                                     scale=SCALING if n == NWT - 1 else 1.0).then_inc(w_hi, 1)
                if n == 1:
                    split_y(0, 0, False)
                    split_y(1, 1, False)
            act.wait_ge(bias_loaded, 48)
            nc.scalar.mul(bt[:, 1:2], bt[:, 0:1], -1.0).then_inc(bt_ready, 1)
            act.wait_ge(bt_ready, 1)
            split_xT(0)
            windows(act, window)

        @block.vector
        def _(dve):
            def layernorm(i, k, src, dst, step, ready):
                base = LN_STEPS * i
                for h in range(2):
                    nc.vector.bn_stats(stats[:, k, h, :], src[:, h * ST:(h + 1) * ST]).then_inc(step, 1)
                dve.wait_ge(step, base + 2)
                dve.sem_inc(stats_seen, 1)
                nc.vector.bn_aggr(mv[:, k, :], stats[:, k, :, :]).then_inc(step, 1)
                dve.wait_ge(step, base + 3)
                dve.wait_ge(rstd_ready[k], i + 1)
                nc.vector.tensor_scalar(dst, src, mv[:, k, 0:1], rstd[:, k:k + 1], ALU.subtract,
                                        ALU.mult).then_inc(ready, 1)

            def first_norm(i, par, reuse):
                dve.wait_ge(xb_ready, i + 1)
                for h in range(2):
                    dve.wait_ge(proj_done, 2 * i + h + 1)
                    cols = slice(h * ST, (h + 1) * ST)
                    nc.vector.tensor_tensor(res[:, 0, cols], ps_a[h][:], xt[:, par, cols], ALU.add).then_inc(res1_ready, 1)
                dve.wait_ge(res1_ready, 2 * i + 2)
                if reuse:
                    dve.wait_ge(xT_done, 2 * i - 2)
                    dve.wait_ge(x1b_ready, i - 1)
                layernorm(i, 0, res[:, 0, :], x1[:, par, :], ln1_step, x1_ready)

            def second_norm(i, par, reuse):
                dve.wait_ge(x1b_ready, i + 1)
                dve.wait_ge(base_done, i + 1)
                for n, (a, b) in enumerate(BANKS):
                    b = min(b, DM)
                    nc.vector.tensor_tensor(res[:, 1, a:b], ps_f[par][n][:, 0:b - a], x1b[:, par, a:b],
                                            ALU.add).then_inc(res2_ready, 1)
                dve.wait_ge(res2_ready, 3 * i + 3)
                if reuse:
                    dve.wait_ge(stored[par], 8 * (i - par))
                layernorm(i, 1, res[:, 1, :], ot[:, par, :], ln2_step, out_ready)

            def split_y(i, par, reuse):
                dve.wait_ge(y_hi, i + 1)
                nc.vector.tensor_tensor(ys[:, par, LO, :, :], yr[:, par, :, :], ys[:, par, HI, :, :].bitcast(F32),
                                        ALU.subtract).then_inc(y_lo, 1)

            def gate(i, par):
                base = GATE_STEPS * i
                dve.wait_ge(gate_done, i + 1)
                nc.vector.tensor_copy(hg[:], ps_f[par][2][:, P:LAST]).then_inc(hg_ready, 1)
                dve.wait_ge(hg_ready, i + 1)
                nc.vector.tensor_reduce(ngm[:], hg[:, ER:ER + EXPERTS], AX_X, ALU.max, negate=True).then_inc(ngm_ready, 1)
                dve.wait_ge(ge_ready, 2 * i + 2)
                nc.vector.tensor_scalar(den[:, 1:2], den[:, 1:2], 1.0, 1.0 / MAX_THRESHOLD, ALU.add,
                                        ALU.mult).then_inc(gate_step, 1)
                dve.wait_ge(gate_step, base + 1)
                nc.vector.reciprocal(inv[:], den[:]).then_inc(gate_step, 1)
                dve.wait_ge(gate_step, base + 2)
                nc.vector.tensor_scalar(adapted[:], ge[:], inv[:, 0:1], inv[:, 1:2], ALU.mult,
                                        ALU.subtract).then_inc(gate_step, 1)
                dve.wait_ge(gate_step, base + 3)
                nc.vector.tensor_scalar(wts[:], adapted[:], 0.0, None, ALU.max).then_inc(gate_step, 1)
                dve.wait_ge(gate_step, base + 4)
                nc.vector.tensor_reduce(wsum[:, 0:1], wts[:], AX_X, ALU.add).then_inc(gate_step, 1)
                dve.wait_ge(gate_step, base + 5)
                nc.vector.scalar_tensor_tensor(out=wsum[:, 1:2], in0=wsum[:, 0:1], scalar=0.0, in1=wsum[:, 0:1],
                                               op0=ALU.is_equal, op1=ALU.add).then_inc(gate_step, 1)
                dve.wait_ge(gate_step, base + 6)
                nc.vector.reciprocal(wsum[:, 2:3], wsum[:, 1:2]).then_inc(gate_step, 1)
                dve.wait_ge(gate_step, base + 7)
                nc.vector.scalar_tensor_tensor(
                    out=hw[:].rearrange("p (e r) -> p e r", e=EXPERTS),
                    in0=hg[:, 0:ER].rearrange("p (e r) -> p e r", e=EXPERTS), scalar=wsum[:, 2:3],
                    in1=wts[:].unsqueeze(2).broadcast_to([P, EXPERTS, RANK]),
                    op0=ALU.mult, op1=ALU.mult).then_inc(hw_ready, 1)

            def split_hT(i, par):
                dve.wait_ge(hT_hi, i + 1)
                nc.vector.tensor_tensor(hT[:, LO, :], ps_f[par][2][:, HT0:HT0 + P], hT[:, HI, :].bitcast(F32),
                                        ALU.subtract).then_inc(hT_lo, 1)

            def split_xT(i):
                for h in range(2):
                    dve.wait_ge(xT_hi, 2 * i + h + 1)
                    part = slice(4 * h, 4 * h + 4)
                    nc.vector.tensor_tensor(x1T[:, LO, part, :], ps_a[h][:].rearrange("p (c n) -> p c n", c=4),
                                            x1T[:, HI, part, :].bitcast(F32), ALU.subtract).then_inc(xT_lo, 1)

            def window(i, par, n):
                if not last(n, 1):
                    first_norm(i + 1, 1 - par, n != 0)
                if not last(n, 2):
                    split_y(i + 2, par, True)
                gate(i, par)
                if n != 0:
                    second_norm(i - 1, 1 - par, n is None or n >= 3)
                split_hT(i, par)
                if not last(n, 1):
                    split_xT(i + 1)

            for n, (_, w, cols) in enumerate(weights):
                dve.wait_ge(w_hi, n + 1)
                raw, hi, lo = wraw[:, n % 2, 0:cols], w[:, HI, :].bitcast(F32), w[:, LO, :]
                if n < NWT - 1:
                    nc.vector.tensor_tensor(lo, raw, hi, ALU.subtract).then_inc(w_lo, 1)
                else:
                    nc.vector.scalar_tensor_tensor(out=lo, in0=raw, scalar=SCALING, in1=hi, op0=ALU.mult,
                                                   op1=ALU.subtract).then_inc(w_lo, 1)
                if n == 1:
                    split_y(0, 0, False)
                    split_y(1, 1, False)
            first_norm(0, 0, False)
            split_xT(0)
            windows(dve, window)
            second_norm(NBLK - 1, 1, True)

        @block.tensor
        def _(pe):
            def project(i, par, first):
                pe.wait_ge(y_lo, i + 1)
                if not first:
                    pe.wait_ge(xT_lo, 2 * i)
                for h in range(2):
                    n = 0
                    for kc in range(KC):
                        for a, b in PASSES:
                            mm = nc.tensor.matmul(ps_a[h][:], ys[:, par, a, kc, :], wp[:, kc, b, h * ST:(h + 1) * ST],
                                                  start=(n == 0), stop=(n == 5))
                            n += 1
                    mm.then_inc(proj_done, 1)

            def transpose_x1(i, par):
                pe.wait_ge(x1_ready, i + 1)
                for h in range(2):
                    for c in range(4):
                        mm = nc.tensor.transpose(ps_a[h][:, c * P:(c + 1) * P],
                                                 x1[:, par, (4 * h + c) * P:(4 * h + c + 1) * P], ident[:])
                    mm.then_inc(xT_done, 1)

            def base(i, par, reuse):
                pe.wait_ge(xT_lo, 2 * i + 2)
                if reuse:
                    pe.wait_ge(res2_ready, 3 * (i - 1))
                for n in (2, 0, 1):
                    a0, b0 = BANKS[n]
                    for kc in range(CC):
                        for k, (a, b) in enumerate(PASSES):
                            mm = nc.tensor.matmul(ps_f[par][n][:, 0:b0 - a0], x1T[:, a, kc, :], wf[:, kc, b, a0:b0],
                                                  start=(kc == 0 and k == 0), stop=(n == 2 and kc == CC - 1 and k == 2),
                                                  skip_group_check=True)
                    if n == 2:
                        mm.then_inc(gate_done, 1)

            def transpose_h(i, par):
                pe.wait_ge(hw_ready, i + 1)
                nc.tensor.matmul(ps_f[par][2][:, HT0:HT0 + P], hw[:], ident[:], is_transpose=True, start=False,
                                 stop=True, skip_group_check=True).then_inc(hT_done, 1)

            def experts(i, par):
                pe.wait_ge(hT_lo, i + 1)
                for n, (a0, b0) in enumerate(BANKS):
                    b0 = min(b0, DM)
                    for k, (a, b) in enumerate(PASSES):
                        mm = nc.tensor.matmul(ps_f[par][n][:, 0:b0 - a0], hT[:, a, :], wb[:, b, a0:b0],
                                              start=False, stop=(k == 2), skip_group_check=True)
                mm.then_inc(base_done, 1)

            def window(i, par, n):
                base(i, par, n is None or n >= 2)
                transpose_h(i, par)
                if not last(n, 1):
                    transpose_x1(i + 1, 1 - par)
                experts(i, par)
                if not last(n, 2):
                    project(i + 2, par, False)

            pe.wait_ge(w_lo, KC)
            project(0, 0, True)
            pe.wait_ge(id_ready, 1)
            transpose_x1(0, 0)
            project(1, 1, False)
            pe.wait_ge(w_lo, NWT)
            windows(pe, window)


def build(nc, ins, out):
    convT = nc.dram_tensor("convT_scratch", [NST, P, CF, ST], F32).ap()
    yT = nc.dram_tensor("yT_scratch", [P, KC, TOK], F32).ap()
    conv_phase(nc, ins["xT"], ins["conv_w"], ins["conv_b"], convT)
    attention_phase(nc, convT, ins["attn_w"], ins["q_bias"], ins["k_bias"], ins["v_bias"], ins["o_bias"],
                    TileColumns(yT, ST))
    ffn_phase(nc, ins["x"], TileColumns(yT, P), ins["proj_w"], ins["proj_b"], ins["ffn_w"], ins["lora_b"],
              ins["b_base"], ins["b_thr"], out)


class TileColumns:

    def __init__(self, ap, width):
        self.ap, self.width = ap, width

    def __getitem__(self, t):
        return self.ap[:, :, bass.ds(t * self.width, self.width)]


def kernel(**inputs):
    import concourse.bacc as bacc
    from concourse.bass_utils import run_bass_kernel_spmd

    a = {k: np.asarray(v) for k, v in inputs.items()}
    x = a["L0_attn_inputs"]
    padded = np.zeros((BATCH, DM, SEQ + TAPS - 1), x.dtype)
    padded[:, :, 1:SEQ + 1] = x.transpose(0, 2, 1)
    xT = np.stack([padded[t // ST_SEQ, :, (t % ST_SEQ) * ST:(t % ST_SEQ) * ST + WIN] for t in range(NST)])

    def chunks(w):
        return w.reshape(-1, P, w.shape[-1]).transpose(1, 0, 2)

    def columns(b):
        return b.reshape(-1, P).T

    w_in = [chunks(a[f"L0_attn_w{n}"].reshape(WB, HE)) for n in "qkv"]
    attn_w = np.stack([w.reshape(P, -1) for w in w_in + [chunks(a["L0_attn_wo"].reshape(HE, WB))]])
    ffn_w = np.concatenate([a["L0_ffn_W_base"], a["L0_ffn_A"].reshape(ER, DM), a["L0_ffn_W_gate"],
                            a["L0_ffn_W_thr"], np.zeros((1, DM), x.dtype)]).T
    arrays = {
        "xT": xT.reshape(NST, CC, P, WIN),
        "conv_w": a["L0_attn_conv_w"].reshape(TAPS, CC, P, 3 * WB).transpose(1, 2, 0, 3),
        "conv_b": columns(a["L0_attn_conv_b"]),
        "attn_w": attn_w,
        "q_bias": columns(a["L0_attn_bq"]),
        "k_bias": columns(a["L0_attn_bk"]),
        "v_bias": a["L0_attn_bv"].reshape(HE),
        "o_bias": columns(a["L0_attn_bo"]),
        "x": x.reshape(NBLK, P, DM),
        "proj_w": a["L0_attn_proj_w"].reshape(KC, P, DM),
        "proj_b": a["L0_attn_proj_b"],
        "ffn_w": ffn_w.reshape(CC, P, WCOLS),
        "lora_b": a["L0_ffn_B"].transpose(0, 2, 1).reshape(ER, DM),
        "b_base": a["L0_ffn_b_base"],
        "b_thr": a["L0_ffn_b_thr"],
    }
    arrays = {k: np.ascontiguousarray(v) for k, v in arrays.items()}
    nc = bacc.Bacc("TRN2", target_bir_lowering=False, num_devices=1)
    ins = {k: nc.dram_tensor(f"in_{k}", v.shape, mybir.dt.from_np(v.dtype), kind="ExternalInput").ap() for k, v in arrays.items()}
    out = nc.dram_tensor("out", [NBLK, P, DM], F32, kind="ExternalOutput").ap()
    build(nc, ins, out)
    result = run_bass_kernel_spmd(nc, [{f"in_{k}": v for k, v in arrays.items()}], core_ids=[0])
    return result.results[0]["out"].reshape(BATCH, SEQ, DM)
```

```python
from contextlib import ExitStack

import numpy as np
import concourse.bass as bass
from concourse import mybir

F32 = mybir.dt.float32
F32R = mybir.dt.float32r
ALU = mybir.AluOpType
ACT = mybir.ActivationFunctionType
AX_X = mybir.AxisListType.X

P = 128
BATCH, SEQ, DM = 2, 2048, 1024
TOK = BATCH * SEQ
TAPS = 3
WB = 256
HEADS, DH = 16, 64
HE = HEADS * DH
EXPERTS, RANK = 8, 16
ER = EXPERTS * RANK
ST = 512
NST = TOK // ST
ST_SEQ = SEQ // ST
BLK = ST // P
NBLK = TOK // P
CC = DM // P
CF = 3 * WB // P
KC = WB // P
HP = HEADS // 2
WIN = ST + TAPS - 1
XS = 4
STAGES = 3
WCOLS = DM + ER + EXPERTS + 2
BANKS = ((0, 512), (512, 896), (896, WCOLS))
SWEEPS = 2
UNITS = SWEEPS * NST
SF = CF // SWEEPS
PROD = TAPS + 1
ARENA = CC * 2 * PROD * SF * P
LAST = BANKS[2][1] - BANKS[2][0]
EPS = 1e-5
SCORE_SCALE = 1.0 / 8.0
MASKED = -1e30
LOWEST = -3.0e38
MAX_THRESHOLD, SCALING = 1.0 / 8.0, 2.0

HI, LO = 0, 1
PASSES = ((HI, HI), (HI, LO), (LO, HI))


class AttentionStart:
    V, K, Q = (4, 6), (2, 4), (0, 2)
    WV, WQ, WK, WO = range(4)
    NW = KC * HE

    def __init__(self, ctx, nc):
        def sb(name, shape, dt):
            return ctx.enter_context(nc.sbuf_tensor(name, shape, dt))

        def sem(name):
            return ctx.enter_context(nc.semaphore(name))

        NW, TILE = self.NW, CF * ST
        self.arena = sb("weights", [P, ARENA], F32R)
        self.stages = sb("weight_stage", [P, 2 * WCOLS], F32)
        self.stage = self.stages[:, 0:NW]
        self.craw = sb("conv_tile", [P, CF, ST], F32)
        self.out = sb("features_out", [P, SF, ST], F32)
        self.mask = sb("causal_mask", [P, P], F32)
        self.ident = sb("identity", [P, P], F32)
        self.bq, self.bk = sb("q_bias", [P, HP], F32), sb("k_bias", [P, HP], F32)
        self.bv, self.bo = sb("v_bias_rows", [P, HE], F32), sb("o_bias", [P, KC], F32)
        self.start = [2 * NW * n for n in range(3)] + [6 * NW + 2 * TILE]
        self.w = [self.arena[:, a:a + 2 * NW].rearrange("p (i n) -> p i n", i=2) for a in self.start]
        self.cs = self.arena[:, 6 * NW:6 * NW + 2 * TILE].rearrange("p (i f n) -> p i f n", i=2, f=CF)

        self.bias_loaded = sem("attn_bias_loaded")
        self.stage_loaded = sem("weight_stage_loaded")
        self.wq_loaded = sem("wq_loaded")
        self.w_hi, self.w_lo = sem("attn_w_hi"), sem("attn_w_lo")
        self.zeroed, self.masks = sem("attn_zeroed"), sem("attn_masks")
        self.c_loaded = sem("conv_tile_loaded")
        self.c_hi, self.c_lo = sem("conv_tile_hi"), sem("conv_tile_lo")
        self.stored = sem("stored")


def conv_phase(nc, xT, conv_w, conv_b, convT, attn, attn_w, q_bias, k_bias, v_bias, o_bias):
    COLS = SF * P
    PAIRS = ST // 2
    LAST_UNIT = UNITS - 1
    with ExitStack() as ctx:
        def sb(name, shape, dt):
            return ctx.enter_context(nc.sbuf_tensor(name, shape, dt))

        def sem(name):
            return ctx.enter_context(nc.semaphore(name))

        w = attn.arena[:].rearrange("p (c i k n) -> p c i k n", c=CC, i=2, k=PROD)
        wraw = sb("conv_w_raw", [P, 2, TAPS, COLS], F32)
        wq_raw = wraw[:].rearrange("p i k n -> p (i k n)")[:, 0:attn.NW]
        wsum = sb("conv_w_sum", [P, COLS], F32)
        wmix = sb("conv_w_mixed", [P, 2, 2, COLS], F32)
        xraw = sb("x_raw", [P, XS, 2, PAIRS + 1], F32)
        xmix = sb("x_mixed", [P, 2, PROD, PAIRS], F32)
        xs = sb("x_split", [P, XS, 2, PROD, PAIRS], F32R)
        mid = sb("conv_mid", [P, SF, 2, PAIRS], F32)
        midmix = sb("conv_mid_mixed", [P, SF, 2, PAIRS], F32)
        out = attn.out
        bias = sb("conv_bias", [P, CF], F32)
        acc = [[ctx.enter_context(nc.psum_tensor(f"conv_acc{f}{i}", [P, 2, PAIRS], F32)) for i in range(2)]
               for f in range(SF)]

        bias_loaded = sem("conv_bias_loaded")
        w_loaded = [sem(f"conv_w_loaded{i}") for i in range(2)]
        w_sum, w_mix = sem("conv_w_summed"), sem("conv_w_mixed")
        w_hi, w_lo = sem("conv_w_hi"), sem("conv_w_lo")
        x_loaded = [sem(f"x_loaded{i}") for i in range(XS)]
        x_mix, x_hi, x_lo = sem("x_mixed"), sem("x_hi"), sem("x_lo")
        x_used = sem("x_used")
        acc_done = sem("conv_acc_done")
        mid_ready, mid_mixed = sem("conv_mid_ready"), sem("conv_mid_mixed")
        out_ready = sem("conv_out_ready")
        stored = attn.stored

        def wait_free(eng, a, b):
            wait_used(eng, LAST_UNIT, (b - 1) * CC // ARENA)

        def wait_used(eng, u, c):
            if c == CC - 1:
                eng.wait_ge(acc_done, SF * (u + 1))
            else:
                eng.wait_ge(x_used, (CC - 1) * u + c + 1)

        def wait_slot(eng, u, c):
            if c >= XS:
                wait_used(eng, u, c - XS)
            elif not (isinstance(u, int) and u == 0):
                wait_used(eng, u - 1, c + CC - XS)

        block = ctx.enter_context(nc.Block())

        @block.sync
        def _(sp):
            def unit(t, sweep, u):
                for c in range(CC):
                    if c >= XS or not (isinstance(u, int) and u == 0):
                        sp.wait_ge(x_mix, CC * u + c - XS + 1)
                    sp.dma_start(xraw[:, c % XS, :, :], xT[t, c]).then_inc(x_loaded[c % XS], 16)
                    if sweep is not None:
                        n = CC * sweep + c
                        if n >= 2:
                            sp.wait_ge(w_lo, 2 * (n - 1))
                        sp.dma_start(wraw[:, n % 2, :, :], conv_w[sweep, c]).then_inc(w_loaded[n % 2], 16)
                    if c == CC - 1 and not (isinstance(u, int) and u == 0):
                        store(u - 1)

            def store(u):
                sp.wait_ge(out_ready, SF * u + SF)
                sp.dma_start(convT[u], out[:]).then_inc(stored, 16)

            sp.dma_start(bias[:], conv_b).then_inc(bias_loaded, 16)
            for sweep in range(SWEEPS):
                unit(0, sweep, NST * sweep)
                with sp.Fori(1, NST - 1) as t:
                    unit(t, None, NST * sweep + t)
                if sweep == SWEEPS - 1:
                    sp.dma_start(attn.stage, attn_w[attn.WV]).then_inc(attn.stage_loaded, 16)
                    sp.wait_ge(w_lo, 2 * SWEEPS * CC)
                    sp.dma_start(wq_raw, attn_w[attn.WQ]).then_inc(attn.wq_loaded, 16)
                    sp.wait_ge(stored, 16 * (NST + 1))
                    for i in range(SWEEPS):
                        sp.dma_start(attn.craw[:, i * SF:(i + 1) * SF, :], convT[i * NST]).then_inc(attn.c_loaded, 16)
                    for b, src in ((attn.bq, q_bias), (attn.bk, k_bias), (attn.bv, v_bias.partition_broadcast(P)),
                                   (attn.bo, o_bias)):
                        sp.dma_start(b[:], src).then_inc(attn.bias_loaded, 16)
                unit(NST - 1, None, NST * sweep + NST - 1)
            for n, before in ((attn.WK, attn.WV), (attn.WO, attn.WK)):
                sp.wait_ge(attn.w_lo, before + 1)
                sp.dma_start(attn.stage, attn_w[n]).then_inc(attn.stage_loaded, 16)
            store(LAST_UNIT)

        @block.gpsimd
        def _(pool):
            nc.gpsimd.memset(attn.mask[:], 0.0).then_inc(attn.zeroed, 1)
            nc.gpsimd.memset(attn.ident[:], 0.0).then_inc(attn.zeroed, 1)
            for n in range(SWEEPS * CC):
                raw, mix = wraw[:, n % 2, :, :], wmix[:, n % 2, :, :]
                pool.wait_ge(w_loaded[n % 2], 16 * (n // 2 + 1))
                if n > 0:
                    pool.wait_ge(w_mix, 2 * n)
                nc.gpsimd.tensor_tensor(wsum[:], raw[:, 0, :], raw[:, 2, :], ALU.add).then_inc(w_sum, 1)
                pool.wait_ge(w_sum, n + 1)
                if n > 1:
                    pool.wait_ge(w_lo, 2 * (n - 1))
                nc.gpsimd.tensor_tensor(mix[:, 0, :], wsum[:], raw[:, 1, :], ALU.add).then_inc(w_mix, 1)
                nc.gpsimd.tensor_tensor(mix[:, 1, :], wsum[:], raw[:, 1, :], ALU.subtract).then_inc(w_mix, 1)
            pool.wait_ge(attn.zeroed, 2)
            nc.gpsimd.affine_select(out=attn.mask[:], in_=attn.mask[:], compare_op=ALU.is_ge, fill=MASKED, base=0,
                                    pattern=[[-1, P]], channel_multiplier=1).then_inc(attn.masks, 1)
            nc.gpsimd.affine_select(out=attn.ident[:], in_=attn.ident[:], compare_op=ALU.not_equal, fill=1.0, base=0,
                                    pattern=[[-1, P]], channel_multiplier=1).then_inc(attn.masks, 1)

        @block.scalar
        def _(act):
            def split_weights(n, c, i):
                if n >= CC:
                    wait_used(act, NST - 1, c)
                if i == 0:
                    act.wait_ge(w_loaded[n % 2], 16 * (n // 2 + 1))
                    nc.scalar.activation(w[:, c, HI, 0:2, :], wraw[:, n % 2, 0:TAPS:2, :], ACT.Copy).then_inc(w_hi, 1)
                else:
                    act.wait_ge(w_mix, 2 * n + 2)
                    nc.scalar.activation(w[:, c, HI, 2:4, :], wmix[:, n % 2, :, :], ACT.Copy, scale=0.5).then_inc(w_hi, 1)

            def split_x(u, c):
                act.wait_ge(x_mix, CC * u + c + 1)
                wait_slot(act, u, c)
                nc.scalar.activation(xs[:, c % XS, HI, :, :], xmix[:, c % 2, :, :], ACT.Copy).then_inc(x_hi, 1)

            def copy_mid(u, sweep):
                if isinstance(u, int) and u == 0:
                    act.wait_ge(bias_loaded, 16)
                for f in range(SF):
                    act.wait_ge(acc_done, SF * u + f + 1)
                    if not (isinstance(u, int) and u == 0):
                        act.wait_ge(mid_mixed, 2 * (SF * (u - 1) + f + 1))
                    nc.scalar.activation(mid[:, f, 0, :], acc[f][1][:, 0, :], ACT.Identity,
                                         bias=bias[:, SF * sweep + f:SF * sweep + f + 1]).then_inc(mid_ready, 1)
                    nc.scalar.activation(mid[:, f, 1, :], acc[f][1][:, 1, :], ACT.Copy).then_inc(mid_ready, 1)

            def unit(u, sweep, before, last=False):
                for c in range(CC):
                    split_x(u, c)
                    if c == (0 if isinstance(u, int) and u % NST == 1 else 2) and before is not None:
                        copy_mid(u - 1, before)
                    if sweep is not None:
                        for i in range(2):
                            split_weights(CC * sweep + c, c, i)
                    if not last:
                        continue
                    if c == CC - 2:
                        split_attn(attn.WV, attn.stage, attn.stage_loaded, 16)
                    if c == CC - 1:
                        split_attn(attn.WQ, wq_raw, attn.wq_loaded, 16)
                        split_attn(attn.WK, attn.stage, attn.stage_loaded, 32)
                        act.wait_ge(attn.c_loaded, 16 * SWEEPS)
                        wait_free(act, attn.start[attn.WK], attn.start[attn.WO])
                        for a, b in (attn.V, attn.K, attn.Q):
                            nc.scalar.activation(attn.cs[:, HI, a:b, :], attn.craw[:, a:b, :], ACT.Copy).then_inc(attn.c_hi, 1)

            def split_attn(n, raw, loaded, count):
                act.wait_ge(loaded, count)
                wait_free(act, attn.start[n], attn.start[n] + 2 * attn.NW)
                nc.scalar.activation(attn.w[n][:, HI, :], raw, ACT.Copy).then_inc(attn.w_hi, 1)

            for sweep in range(SWEEPS):
                unit(NST * sweep, sweep, sweep - 1 if sweep else None)
                unit(NST * sweep + 1, None, sweep)
                with act.Fori(NST * sweep + 2, NST * (sweep + 1) - 1) as u:
                    unit(u, None, sweep)
                unit(NST * (sweep + 1) - 1, None, sweep, sweep == SWEEPS - 1)
            copy_mid(LAST_UNIT, SWEEPS - 1)

        @block.vector
        def _(dve):
            def mix(u, c):
                even, odd, src = xraw[:, c % XS, 0, :], xraw[:, c % XS, 1, :], xraw[:, c % XS, :, :]
                dst = xmix[:, c % 2, :, :]
                if c >= 2 or not (isinstance(u, int) and u == 0):
                    dve.wait_ge(x_lo, CC * u + c - 1)
                dve.wait_ge(x_loaded[c % XS], 16 * (CC // XS * u + c // XS + 1))
                nc.vector.tensor_tensor(dst[:, 0:2, :], src[:, :, 0:PAIRS], src[:, :, 1:PAIRS + 1], ALU.subtract)
                nc.vector.tensor_tensor(dst[:, 2, :], odd[:, 0:PAIRS], even[:, 1:PAIRS + 1], ALU.add)
                nc.vector.tensor_tensor(dst[:, 3, :], even[:, 1:PAIRS + 1], odd[:, 0:PAIRS],
                                        ALU.subtract).then_inc(x_mix, 1)

            def split_x(u, c):
                dve.wait_ge(x_hi, CC * u + c + 1)
                nc.vector.tensor_tensor(xs[:, c % XS, LO, :, :], xmix[:, c % 2, :, :],
                                        xs[:, c % XS, HI, :, :].bitcast(F32), ALU.subtract).then_inc(x_lo, 1)

            def split_weights(n, c):
                dve.wait_ge(w_hi, 2 * n + 1)
                nc.vector.tensor_tensor(w[:, c, LO, 0:2, :], wraw[:, n % 2, 0:TAPS:2, :],
                                        w[:, c, HI, 0:2, :].bitcast(F32), ALU.subtract).then_inc(w_lo, 1)
                dve.wait_ge(w_hi, 2 * n + 2)
                nc.vector.scalar_tensor_tensor(out=w[:, c, LO, 2:4, :], in0=wmix[:, n % 2, :, :], scalar=0.5,
                                               in1=w[:, c, HI, 2:4, :].bitcast(F32), op0=ALU.mult,
                                               op1=ALU.subtract).then_inc(w_lo, 1)

            def finish(u):
                if not (isinstance(u, int) and u == 0):
                    dve.wait_ge(stored, 16 * u)
                for f in range(SF):
                    count = SF * u + f + 1
                    dve.wait_ge(mid_ready, 2 * count)
                    nc.vector.tensor_tensor(midmix[:, f, 0, :], mid[:, f, 0, :], mid[:, f, 1, :],
                                            ALU.add).then_inc(mid_mixed, 1)
                    nc.vector.tensor_tensor(midmix[:, f, 1, :], mid[:, f, 0, :], mid[:, f, 1, :],
                                            ALU.subtract).then_inc(mid_mixed, 1)
                    dve.wait_ge(mid_mixed, 2 * count)
                    nc.vector.tensor_tensor(out[:, f, 0:ST:2], midmix[:, f, 0, :], acc[f][0][:, 0, :], ALU.add)
                    nc.vector.tensor_tensor(out[:, f, 1:ST:2], midmix[:, f, 1, :], acc[f][0][:, 1, :],
                                            ALU.subtract).then_inc(out_ready, 1)

            def unit(u, sweep, last=False):
                for c in range(CC):
                    first = isinstance(u, int) and u == 0 and c == 0
                    if first:
                        split_x(u, c)
                        split_weights(c, c)
                    if c < CC - 1:
                        mix(u, c + 1)
                    elif not last:
                        mix(u + 1, 0)
                    if first:
                        continue
                    split_x(u, c)
                    if c == (0 if isinstance(u, int) and u % NST == 1 else 2) and not (isinstance(u, int) and u == 0):
                        finish(u - 1)
                    if sweep is not None:
                        split_weights(CC * sweep + c, c)
                    if not last:
                        continue
                    if c == CC - 2:
                        split_attn(attn.WV, attn.stage)
                    if c == CC - 1:
                        split_attn(attn.WQ, wq_raw)
                        split_attn(attn.WK, attn.stage)
                        for n, (a, b) in enumerate((attn.V, attn.K, attn.Q)):
                            dve.wait_ge(attn.c_hi, n + 1)
                            nc.vector.tensor_tensor(attn.cs[:, LO, a:b, :], attn.craw[:, a:b, :],
                                                    attn.cs[:, HI, a:b, :].bitcast(F32), ALU.subtract).then_inc(attn.c_lo, 1)

            def split_attn(n, raw):
                dve.wait_ge(attn.w_hi, n + 1)
                nc.vector.tensor_tensor(attn.w[n][:, LO, :], raw, attn.w[n][:, HI, :].bitcast(F32),
                                        ALU.subtract).then_inc(attn.w_lo, 1)

            mix(0, 0)
            for sweep in range(SWEEPS):
                unit(NST * sweep, sweep)
                unit(NST * sweep + 1, None)
                with dve.Fori(NST * sweep + 2, NST * (sweep + 1) - 1) as u:
                    unit(u, None)
                unit(NST * (sweep + 1) - 1, None, sweep == SWEEPS - 1)
            finish(LAST_UNIT)

        @block.tensor
        def _(pe):
            def products(u, c, f, ks):
                for k in ks:
                    for i, (a, b) in enumerate(PASSES):
                        last = nc.tensor.matmul(acc[f][k // 2][:, k % 2, :], w[:, c, a, k, f * P:(f + 1) * P],
                                                xs[:, c % XS, b, k, :], start=(c == 0 and k % 2 == 0 and i == 0),
                                                stop=(c == CC - 1 and k % 2 == 1 and i == 2), skip_group_check=True)
                if c == CC - 1 and PROD - 1 in ks:
                    last.then_inc(acc_done, 1)
                return last

            def unit(u, sweep):
                for c in range(CC):
                    if sweep is not None:
                        pe.wait_ge(w_lo, 2 * (CC * sweep + c) + 1)
                    pe.wait_ge(x_lo, CC * u + c + 1)
                    for f in range(SF):
                        if c == 0 and not (isinstance(u, int) and u == 0):
                            if sweep is None:
                                pe.wait_ge(mid_ready, 2 * (SF * (u - 1) + f + 1))
                                products(u, c, f, (2, 3))
                            pe.wait_ge(out_ready, SF * (u - 1) + f + 1)
                        last = products(u, c, f, (0, 1) if c == 0 or sweep is not None else range(PROD))
                    if sweep is not None:
                        pe.wait_ge(w_lo, 2 * (CC * sweep + c) + 2)
                        for f in range(SF):
                            last = products(u, c, f, (2, 3))
                    if c < CC - 1:
                        last.then_inc(x_used, 1)

            for sweep in range(SWEEPS):
                unit(NST * sweep, sweep)
                with pe.Fori(NST * sweep + 1, NST * (sweep + 1)) as u:
                    unit(u, None)


class FfnStart:
    LATE = 2

    def __init__(self, ctx, nc, attn, proj_w, ffn_w, lora_b):
        def sb(name, shape, dt):
            return ctx.enter_context(nc.sbuf_tensor(name, shape, dt))

        def sem(name):
            return ctx.enter_context(nc.semaphore(name))

        def parts(a, n):
            return attn.arena[:, a:a + 2 * n].rearrange("p (i n) -> p i n", i=2)

        k_cols, q_cols = 2 * 2 * BLK * 2 * P, 2 * 2 * ST
        pair = sb("q_k_pairs", [P, k_cols + q_cols], F32R)
        self.k = pair[:, 0:k_cols].rearrange("p (i h b j n) -> p i h b j n", i=2, h=2, b=BLK, j=2)
        self.q = pair[:, k_cols:].rearrange("p (i h n) -> p i h n", i=2, h=2)
        wq, kept = attn.start[attn.WQ], CC - self.LATE
        self.wp = [parts(attn.start[attn.WV] + 2 * DM * k, DM) for k in range(KC)]
        self.wf = [parts(wq + 2 * WCOLS * k, WCOLS) for k in range(kept)]
        self.wf += [pair[:, 2 * WCOLS * k:2 * WCOLS * (k + 1)].rearrange("p (i n) -> p i n", i=2) for k in range(self.LATE)]
        self.wb = parts(attn.start[attn.WO] + 2 * attn.NW, DM)
        wo = attn.start[attn.WO]
        self.x1T = attn.arena[:, wo:wo + 4 * DM].rearrange("p (i h k n) -> p i h k n", i=2, h=2, k=CC)
        self.stage = [attn.stages[:, i * WCOLS:(i + 1) * WCOLS] for i in range(2)]
        self.stage.append(sb("weight_stage2", [P, WCOLS], F32)[:])
        f = [(ffn_w[k], self.wf[k], WCOLS) for k in range(CC)]
        p = [(proj_w[k], self.wp[k], DM) for k in range(KC)]
        self.weights = [(lora_b, self.wb, DM)] + p + f
        self.AFTER_V, self.AFTER_QK = 1, 1 + KC
        self.KEPT = len(self.weights) - self.LATE
        raw = attn.craw[:].rearrange("p f n -> p (f n)")
        self.xt = raw[:, 0:2 * DM].rearrange("p (i n) -> p i n", i=2)
        self.yr = raw[:, 2 * DM:2 * DM + 2 * KC * P].rearrange("p (i k n) -> p i k n", i=2, k=KC)
        self.ys = sb("y_split", [P, 2, 2, KC, P], F32R)
        self.pb = sb("proj_b_rows", [P, DM], F32)

        self.w_loaded = [sem(f"ffn_w_loaded{i}") for i in range(STAGES)]
        self.w_hi = sem("ffn_w_hi")
        self.w_lo = [sem(f"ffn_w_lo{n}") for n in range(len(self.weights))]
        self.pb_loaded = sem("proj_b_loaded")
        self.x_loaded = [sem(f"x_tile_loaded{i}") for i in range(2)]
        self.y_loaded = [sem(f"y_loaded{i}") for i in range(2)]
        self.xb_ready = sem("x_plus_bias_ready")
        self.y_hi, self.y_lo = sem("y_hi"), sem("y_lo")
        self.attn_stored = attn.stored
        self.proj_done = sem("proj_done")
        self.res1_ready = sem("res1_ready")

        self.stats = sb("ln_stats", [P, 2, 2, 6], F32)
        self.mv = sb("ln_mean_var", [P, 2, 2], F32)
        self.var_eps, self.rstd = sb("ln_var_eps", [P, 2], F32), sb("ln_rstd", [P, 2], F32)
        self.minus_half, self.eps = sb("minus_half", [P, 1], F32), sb("eps", [P, 1], F32)
        self.consts = sem("ln_consts_ready")
        self.ln_step = [sem(f"ln{k + 1}_step") for k in range(2)]
        self.var_ready = [sem(f"ln{k + 1}_var_ready") for k in range(2)]
        self.rstd_ready = [sem(f"ln{k + 1}_rstd_ready") for k in range(2)]
        self.stats_seen = sem("ln_stats_seen")
        self.x1_ready = sem("x1_ready")
        self.first_x1 = attn.bv

    LN_STEPS = 3

    def project_half(self, nc, i, par, h, bank):
        n = 0
        for kc in range(KC):
            for a, b in PASSES:
                mm = nc.tensor.matmul(bank[:], self.ys[:, par, a, kc, :], self.wp[kc][:, b, h * ST:(h + 1) * ST],
                                      start=(n == 0), stop=(n == 5))
                n += 1
        mm.then_inc(self.proj_done, 1)

    def add_half(self, nc, dve, i, par, h, bank, res):
        if h == 0:
            dve.wait_ge(self.xb_ready, i + 1)
        dve.wait_ge(self.proj_done, 2 * i + h + 1)
        cols = slice(h * ST, (h + 1) * ST)
        nc.vector.tensor_tensor(res[:, cols], bank[:], self.xt[:, par, cols], ALU.add).then_inc(self.res1_ready, 1)

    def ln_stats(self, nc, dve, i, k, src):
        step = self.ln_step[k]
        for h in range(2):
            nc.vector.bn_stats(self.stats[:, k, h, :], src[:, h * ST:(h + 1) * ST]).then_inc(step, 1)
        dve.wait_ge(step, self.LN_STEPS * i + 2)
        dve.sem_inc(self.stats_seen, 1)
        nc.vector.bn_aggr(self.mv[:, k, :], self.stats[:, k, :, :]).then_inc(step, 1)

    def ln_apply(self, nc, dve, i, k, src, dst, ready):
        dve.wait_ge(self.ln_step[k], self.LN_STEPS * i + 3)
        dve.wait_ge(self.rstd_ready[k], i + 1)
        nc.vector.tensor_scalar(dst, src, self.mv[:, k, 0:1], self.rstd[:, k:k + 1], ALU.subtract,
                                ALU.mult).then_inc(ready, 1)

    def inverse_root(self, nc, pool, i, k):
        pool.wait_ge(self.ln_step[k], self.LN_STEPS * i + 3)
        nc.gpsimd.tensor_tensor(self.var_eps[:, k:k + 1], self.mv[:, k, 1:2], self.eps[:], ALU.add).then_inc(self.var_ready[k], 1)
        pool.wait_ge(self.var_ready[k], i + 1)
        nc.gpsimd.tensor_tensor(self.rstd[:, k:k + 1], self.var_eps[:, k:k + 1], self.minus_half[:],
                                ALU.pow).then_inc(self.rstd_ready[k], 1)


def attention_phase(nc, convT, attn, yT, ffn, x, y_blocks, proj_b):
    PAIRS = NST * HP
    with ExitStack() as ctx:
        def sb(name, shape, dt):
            return ctx.enter_context(nc.sbuf_tensor(name, shape, dt))

        def psum(name):
            return ctx.enter_context(nc.psum_tensor(name, [P, ST], F32))

        def sem(name):
            return ctx.enter_context(nc.semaphore(name))

        w, cs, craw = attn.w, attn.cs, attn.craw
        mask, ident = attn.mask, attn.ident
        bq, bk, bv, bo = attn.bq, attn.bk, attn.bv, attn.bo
        v = sb("v_heads", [P, BLK, HE], F32)
        q, k = ffn.q, ffn.k
        probs = sb("scores_and_probs", [P, 2, 2 * BLK, P], F32)
        top = sb("score_max", [P, 2, 2 * BLK], F32)
        ntop = sb("score_neg_max", [P, 2, 2 * BLK], F32)
        total = sb("prob_sum", [P, 2, 2 * BLK], F32)
        inv = sb("prob_inv_sum", [P, 2, 2 * BLK], F32)
        oT = sb("heads_out", [P, 2, 2, ST], F32R)
        probsT = sb("probs_T", [P, 2, ST], F32)
        y = attn.out[:, 0:KC, :]
        ps_qt, ps_kt = psum("ps_q_and_probsT0"), psum("ps_k_and_probsT1")
        ps_s = [psum("ps_scores0"), psum("ps_scores1")]
        ps_o, ps_v = psum("ps_heads_out"), psum("ps_v")
        ps_y = [psum("ps_out0"), psum("ps_out1")]

        def rows(j):
            return slice(j * DH, (j + 1) * DH)

        def wqkv(n, part, kc, cols):
            return w[n][:, part, :].rearrange("p (k n) -> p k n", k=KC)[:, kc, cols]

        def wo(part, s, cols):
            return w[attn.WO][:, part, :].rearrange("p (k n) -> p k n", k=HP)[:, s, cols]

        w_hi, w_lo = attn.w_hi, attn.w_lo
        c_loaded, c_hi, c_lo = attn.c_loaded, attn.c_hi, attn.c_lo
        v_done, v_ready = sem("v_done"), sem("v_ready")
        k_zeroed = sem("k_zeroed")
        qk_done = sem("qk_done")
        q_hi, k_hi = sem("q_hi"), sem("k_hi")
        q_ready, k_ready = sem("q_ready"), sem("k_ready")
        s_done = sem("scores_done")
        scores_seen = sem("scores_seen")
        masked = sem("scores_masked")
        ntop_ready = sem("neg_max_ready")
        exps, inv_ready, normed = sem("exps"), sem("inv_sum_ready"), sem("probs_normed")
        t_done, t0_ready, t1_ready = sem("probsT_done"), sem("probsT0_ready"), sem("probsT1_ready")
        o_done, o_hi, o_lo = sem("heads_out_done"), sem("heads_out_hi"), sem("heads_out_lo")
        y_done, y_ready, stored = sem("attn_out_done"), sem("attn_out_ready"), attn.stored

        block = ctx.enter_context(nc.Block())
        V, K, Q = attn.V, attn.K, attn.Q
        V_SPLIT, QK_SPLIT = 4, 5

        def pair(t, s):
            return HP * t + s

        def exists(t, s):
            return not isinstance(t, int) or 0 <= pair(t, s) < PAIRS

        def tiles(eng, tile):
            tile(0)
            with eng.Fori(1, NST - 1) as t:
                tile(t)
            tile(NST - 1)

        def is_last(t):
            return isinstance(t, int) and t == NST - 1

        FFN_STEPS = ((0,), (), (), (1,), (2,), (3, 4), (5,), (6, 7))
        FFN_END, VECTOR_SHARE = (8,), (4, 8)
        PROJECT_STEP = HP - 2
        first_res = probs[:, 0, :, :].rearrange("p n k -> p (n k)")
        Y_STEP = 2

        def v_group(t, s):
            return pair(t, s) + BLK, s % BLK, slice(ST, 2 * ST) if s < BLK else slice(0, ST)

        @block.sync
        def _(sp):
            def load_conv(t):
                sp.wait_ge(c_lo, 3 * t)
                for sweep in range(2):
                    part = slice(sweep * CF // 2, (sweep + 1) * CF // 2)
                    sp.dma_start(craw[:, part, :], convT[t + sweep * NST]).then_inc(c_loaded, 16)

            def store(t):
                sp.wait_ge(y_ready, KC * t + KC)
                sp.dma_start(yT[t], y).then_inc(stored, 16)

            sp.wait_ge(stored, 16 * UNITS)
            load_conv(1)
            with sp.Fori(1, NST - 1) as t:
                store(t - 1)
                load_conv(t + 1)
            sp.wait_ge(c_lo, 3 * NST)
            sp.wait_ge(stored, 16 * (UNITS + 1))
            for i in range(2):
                sp.dma_start(ffn.yr[:, i, :, :], y_blocks[i]).then_inc(ffn.y_loaded[i], 16)
                sp.dma_start(ffn.xt[:, i, :], x[i]).then_inc(ffn.x_loaded[i], 16)
            sp.dma_start(ffn.pb[:], proj_b.partition_broadcast(P)).then_inc(ffn.pb_loaded, 16)
            for n, (src, _, cols) in enumerate(ffn.weights):
                if n == ffn.AFTER_V:
                    store(NST - 2)
                if n >= STAGES:
                    sp.wait_ge(ffn.w_lo[n - STAGES], 1)
                sp.dma_start(ffn.stage[n % STAGES][:, 0:cols], src).then_inc(ffn.w_loaded[n % STAGES], 16)
            store(NST - 1)

        @block.gpsimd
        def _(pool):
            nc.gpsimd.memset(ffn.minus_half[:], -0.5).then_inc(ffn.consts, 1)
            nc.gpsimd.memset(ffn.eps[:], EPS).then_inc(ffn.consts, 1)
            pool.wait_ge(ffn.consts, 2)
            for i in range(2):
                for j in range(2):
                    nc.gpsimd.memset(k[rows(1 - j), i, :, :, j, :].bitcast(F32), 0.0).then_inc(k_zeroed, 1)
            pool.wait_ge(k_zeroed, 4)
            pool.wait_ge(w_hi, attn.WO + 1)
            nc.gpsimd.tensor_tensor(w[attn.WO][:, LO, :], attn.stage, w[attn.WO][:, HI, :].bitcast(F32),
                                    ALU.subtract).then_inc(w_lo, 1)
            with pool.Fori(1, NST) as t:
                for n, (a, b) in ((0, V), (2, Q)):
                    pool.wait_ge(c_hi, 3 * t + n + 1)
                    pool.wait_ge(c_lo, 3 * t + n)
                    nc.gpsimd.tensor_tensor(cs[:, LO, a:b, :], craw[:, a:b, :], cs[:, HI, a:b, :].bitcast(F32),
                                            ALU.subtract).then_inc(c_lo, 1)
            pool.wait_ge(ffn.pb_loaded, 16)
            for i in range(2):
                pool.wait_ge(ffn.x_loaded[i], 16)
                nc.gpsimd.tensor_tensor(ffn.xt[:, i, :], ffn.xt[:, i, :], ffn.pb[:], ALU.add).then_inc(ffn.xb_ready, 1)
            for n in range(1, ffn.KEPT):
                if n in VECTOR_SHARE:
                    continue
                _, dst, cols = ffn.weights[n]
                if n == ffn.KEPT - 2:
                    ffn.inverse_root(nc, pool, 0, 0)
                pool.wait_ge(ffn.w_hi, n + 1)
                nc.gpsimd.tensor_tensor(dst[:, LO, :], ffn.stage[n % STAGES][:, 0:cols], dst[:, HI, :].bitcast(F32),
                                        ALU.subtract).then_inc(ffn.w_lo[n], 1)

        @block.scalar
        def _(act):
            def split(parts):
                for a, b in parts:
                    nc.scalar.activation(cs[:, HI, a:b, :], craw[:, a:b, :], ACT.Copy).then_inc(c_hi, 1)

            def q_out(g, s):
                act.wait_ge(qk_done, 2 * g + 2)
                nc.scalar.activation(q[:, s % 2, HI, :], ps_qt[:], ACT.Identity, bias=bq[:, s:s + 1]).then_inc(q_hi, 1)

            def k_out(g, s):
                act.wait_ge(qk_done, 2 * g + 1)
                for j in range(2):
                    nc.scalar.activation(k[rows(j), s % 2, HI, :, j, :],
                                         ps_kt[rows(j), :].rearrange("p (b n) -> p b n", b=BLK), ACT.Identity,
                                         bias=bk[rows(j), s:s + 1]).then_inc(k_hi, 1)

            def exp(g, s):
                for h in range(2):
                    act.wait_ge(ntop_ready, 2 * g + h + 1)
                    for i in range(h * BLK, (h + 1) * BLK):
                        last = nc.scalar.activation(probs[:, s % 2, i, :], probs[:, s % 2, i, :], ACT.Exp,
                                                    bias=ntop[:, s % 2, i:i + 1], scale=SCORE_SCALE,
                                                    accum_out=total[:, s % 2, i:i + 1])
                last.then_inc(exps, 1)

            def probsT_out(g):
                act.wait_ge(t_done, 2 * g + 1)
                nc.scalar.activation(probsT[:, 0, :], ps_qt[:], ACT.Copy).then_inc(t0_ready, 1)

            def heads_out(g, s):
                act.wait_ge(o_done, g + 1)
                nc.scalar.activation(oT[:, s % 2, HI, :], ps_o[:], ACT.Copy).then_inc(o_hi, 1)

            def out(t):
                act.wait_ge(stored, 16 * (UNITS + t))
                for m in range(KC):
                    act.wait_ge(y_done, KC * t + m + 1)
                    nc.scalar.activation(y[:, m, :], ps_y[m][:], ACT.Identity, bias=bo[:, m:m + 1]).then_inc(y_ready, 1)

            def split_ffn(n):
                _, dst, cols = ffn.weights[n]
                act.wait_ge(ffn.w_loaded[n % STAGES], 16 * (n // STAGES + 1))
                if n >= ffn.AFTER_V:
                    act.wait_ge(v_done, PAIRS)
                if n >= ffn.AFTER_QK:
                    act.wait_ge(qk_done, 2 * PAIRS)
                nc.scalar.activation(dst[:, HI, :], ffn.stage[n % STAGES][:, 0:cols], ACT.Copy,
                                     scale=SCALING if n == 0 else 1.0).then_inc(ffn.w_hi, 1)

            def split_y():
                for i in range(2):
                    act.wait_ge(ffn.y_loaded[i], 16)
                    nc.scalar.activation(ffn.ys[:, i, HI, :, :], ffn.yr[:, i, :, :], ACT.Copy).then_inc(ffn.y_hi, 1)

            def tile(t):
                for s in range(HP):
                    if s == V_SPLIT and exists(t, HP):
                        act.wait_ge(c_loaded, 32 * (t + 2))
                        act.wait_ge(v_done, pair(t, s) + BLK)
                        split([V])
                    if s == 2 and exists(t, -1):
                        out(t - 1)
                    if exists(t, s + 2):
                        k_out(pair(t, s + 2), (s + 2) % HP)
                        q_out(pair(t, s + 2), (s + 2) % HP)
                    if s == QK_SPLIT and exists(t, HP):
                        act.wait_ge(qk_done, 2 * pair(t, HP))
                        split([K, Q])
                    if exists(t, s - 1):
                        heads_out(pair(t, s - 1), s - 1)
                    probsT_out(pair(t, s))
                    if exists(t, s + 1):
                        exp(pair(t, s + 1), s + 1)
                    if is_last(t):
                        for n in FFN_STEPS[s]:
                            split_ffn(n)
                        if s == Y_STEP:
                            split_y()

            act.wait_ge(attn.bias_loaded, 64)
            for g in range(2):
                k_out(g, g)
                q_out(g, g)
            act.wait_ge(attn.stage_loaded, 48)
            nc.scalar.activation(w[attn.WO][:, HI, :], attn.stage, ACT.Copy).then_inc(w_hi, 1)
            exp(0, 0)
            tiles(act, tile)
            heads_out(PAIRS - 1, HP - 1)
            for n in FFN_END:
                split_ffn(n)
            out(NST - 1)

        @block.vector
        def _(dve):
            def split_k(t):
                a, b = K
                dve.wait_ge(c_hi, 3 * t + 2)
                dve.wait_ge(c_lo, 3 * t + 1)
                nc.vector.tensor_tensor(cs[:, LO, a:b, :], craw[:, a:b, :], cs[:, HI, a:b, :].bitcast(F32),
                                        ALU.subtract).then_inc(c_lo, 1)

            def v_out(n, b, cols):
                dve.wait_ge(v_done, n + 1)
                nc.vector.tensor_tensor(v[:, b, cols], ps_v[:], bv[:, cols], ALU.add).then_inc(v_ready, 1)

            def qk_out(g, s):
                for j in range(2):
                    dve.wait_ge(k_hi, 2 * g + j + 1)
                    last = nc.vector.scalar_tensor_tensor(
                        out=k[rows(j), s % 2, LO, :, j, :], in0=ps_kt[rows(j), :].rearrange("p (b n) -> p b n", b=BLK),
                        scalar=bk[rows(j), s:s + 1], in1=k[rows(j), s % 2, HI, :, j, :].bitcast(F32),
                        op0=ALU.add, op1=ALU.subtract)
                last.then_inc(k_ready, 1)
                dve.wait_ge(q_hi, g + 1)
                nc.vector.scalar_tensor_tensor(out=q[:, s % 2, LO, :], in0=ps_qt[:], scalar=bq[:, s:s + 1],
                                               in1=q[:, s % 2, HI, :].bitcast(F32), op0=ALU.add,
                                               op1=ALU.subtract).then_inc(q_ready, 1)

            def mask_max(g, s):
                for h in range(2):
                    dve.wait_ge(s_done, 2 * g + h + 1)
                    dve.sem_inc(scores_seen, 1)
                    half = slice(h * BLK, (h + 1) * BLK)
                    for n in range(BLK):
                        i = h * BLK + n
                        last = nc.vector.tensor_tensor_reduce(
                            out=probs[:, s % 2, i, :], in0=ps_s[h][:, n * P:(n + 1) * P], in1=mask[:], scale=1.0,
                            scalar=LOWEST, op0=ALU.add, op1=ALU.max, accum_out=top[:, s % 2, i:i + 1])
                    last.then_inc(masked, 1)
                    dve.wait_ge(masked, 2 * g + h + 1)
                    nc.vector.tensor_scalar(ntop[:, s % 2, half], top[:, s % 2, half], -SCORE_SCALE, None,
                                            ALU.mult).then_inc(ntop_ready, 1)

            def normalize(g, s):
                dve.wait_ge(exps, g + 1)
                nc.vector.reciprocal(inv[:, s % 2, :], total[:, s % 2, :]).then_inc(inv_ready, 1)
                dve.wait_ge(inv_ready, g + 1)
                nc.vector.tensor_tensor(probs[:, s % 2, :, :], probs[:, s % 2, :, :],
                                        inv[:, s % 2, :].unsqueeze(2).broadcast_to([P, 2 * BLK, P]),
                                        ALU.mult).then_inc(normed, 1)

            def probsT_out(g):
                dve.wait_ge(t_done, 2 * g + 2)
                nc.vector.tensor_copy(probsT[:, 1, :], ps_kt[:]).then_inc(t1_ready, 1)

            def heads_out(g, s):
                dve.wait_ge(o_hi, g + 1)
                nc.vector.tensor_tensor(oT[:, s % 2, LO, :], ps_o[:], oT[:, s % 2, HI, :].bitcast(F32),
                                        ALU.subtract).then_inc(o_lo, 1)

            def split_ffn(n):
                _, dst, cols = ffn.weights[n]
                dve.wait_ge(ffn.w_hi, n + 1)
                nc.vector.tensor_tensor(dst[:, LO, :], ffn.stage[n % STAGES][:, 0:cols], dst[:, HI, :].bitcast(F32),
                                        ALU.subtract).then_inc(ffn.w_lo[n], 1)

            def split_b():
                raw, hi, lo = ffn.stage[0][:, 0:DM], ffn.wb[:, HI, :].bitcast(F32), ffn.wb[:, LO, :]
                dve.wait_ge(ffn.w_hi, 1)
                nc.vector.scalar_tensor_tensor(out=lo, in0=raw, scalar=SCALING, in1=hi, op0=ALU.mult,
                                               op1=ALU.subtract).then_inc(ffn.w_lo[0], 1)

            def split_y():
                for i in range(2):
                    dve.wait_ge(ffn.y_hi, i + 1)
                    nc.vector.tensor_tensor(ffn.ys[:, i, LO, :, :], ffn.yr[:, i, :, :],
                                            ffn.ys[:, i, HI, :, :].bitcast(F32), ALU.subtract).then_inc(ffn.y_lo, 1)

            def tile(t):
                for s in range(HP):
                    normalize(pair(t, s), s)
                    if exists(t, s + 2):
                        qk_out(pair(t, s + 2), (s + 2) % HP)
                    if exists(t, s + 1):
                        mask_max(pair(t, s + 1), s + 1)
                    if s == QK_SPLIT and exists(t, HP):
                        split_k(t + 1)
                    probsT_out(pair(t, s))
                    if s < BLK or exists(t, HP):
                        v_out(*v_group(t, s))
                    if exists(t, s - 1):
                        heads_out(pair(t, s - 1), s - 1)
                    if is_last(t):
                        if s == 0:
                            split_b()
                        if s >= PROJECT_STEP:
                            ffn.add_half(nc, dve, 0, 0, s - PROJECT_STEP, ps_v, first_res)
                        if s == PROJECT_STEP:
                            split_ffn(VECTOR_SHARE[0])
                        if s == Y_STEP:
                            split_y()

            dve.wait_ge(attn.bias_loaded, 64)
            v_out(0, 0, slice(0, ST))
            qk_out(0, 0)
            v_out(1, 1, slice(0, ST))
            qk_out(1, 1)
            dve.wait_ge(attn.masks, 2)
            mask_max(0, 0)
            for b in range(2, BLK):
                v_out(b, b, slice(0, ST))
            tiles(dve, tile)
            dve.wait_ge(ffn.res1_ready, 2)
            ffn.ln_stats(nc, dve, 0, 0, first_res)
            heads_out(PAIRS - 1, HP - 1)
            dve.wait_ge(v_ready, PAIRS)
            ffn.ln_apply(nc, dve, 0, 0, first_res, ffn.first_x1[:], ffn.x1_ready)
            split_ffn(VECTOR_SHARE[1])

        @block.tensor
        def _(pe):
            def project_v(n, b, cols):
                if not (isinstance(n, int) and n == 0):
                    pe.wait_ge(v_ready, n)
                i = 0
                for kc in range(KC):
                    for a, c in PASSES:
                        last = nc.tensor.matmul(ps_v[:], cs[:, a, V[0] + kc, b * P:(b + 1) * P], wqkv(attn.WV, c, kc, cols),
                                                start=(i == 0), stop=(i == 5))
                        i += 1
                last.then_inc(v_done, 1)

            def project_qk(g, s, copied=None, count=0, t=None):
                for n, (weight, part, out) in enumerate(((attn.WK, K, ps_kt), (attn.WQ, Q, ps_qt))):
                    if copied is not None:
                        pe.wait_ge(copied[n], count)
                    if t is not None:
                        pe.wait_ge(c_lo, 3 * t + n + 2)
                    i = 0
                    for kc in range(KC):
                        for a, c in PASSES:
                            last = nc.tensor.matmul(out[:], wqkv(weight, a, kc, slice(s * P, (s + 1) * P)),
                                                    cs[:, c, part[0] + kc, :], start=(i == 0), stop=(i == 5))
                            i += 1
                    last.then_inc(qk_done, 1)

            def make_scores(g, s, first):
                pe.wait_ge(q_ready, g + 1)
                pe.wait_ge(k_ready, g + 1)
                if not first:
                    pe.wait_ge(masked, 2 * g)
                for b in range(BLK):
                    for i, (a, c) in enumerate(PASSES):
                        last = nc.tensor.matmul(ps_s[b // 2][:, b % 2 * 2 * P:(b % 2 + 1) * 2 * P],
                                                q[:, s % 2, a, b * P:(b + 1) * P], k[:, s % 2, c, b, :, :],
                                                start=(i == 0), stop=(i == 2))
                    if b % 2 == 1:
                        last.then_inc(s_done, 1)

            def transpose_probs(g, s, projected):
                pe.wait_ge(normed, g + 1)
                pe.wait_ge(q_ready, projected)
                pe.wait_ge(k_ready, projected)
                for j, out in enumerate((ps_qt, ps_kt)):
                    for b in range(BLK):
                        last = nc.tensor.transpose(out[:, b * P:(b + 1) * P], probs[:, s % 2, 2 * b + j, :], ident[:])
                    last.then_inc(t_done, 1)

            def weigh_v(g, s, groups, first):
                pe.wait_ge(t0_ready, g + 1)
                pe.wait_ge(t1_ready, g + 1)
                pe.wait_ge(v_ready, groups)
                if not first:
                    pe.wait_ge(o_lo, g)
                for j in range(2):
                    head = slice((2 * s + j) * DH, (2 * s + j + 1) * DH)
                    for b in range(BLK):
                        cols = slice(b * P, (b + 1) * P)
                        last = nc.tensor.matmul(ps_o[j * DH:(j + 1) * DH, cols], v[:, b, head], probsT[:, j, cols],
                                                start=True, stop=True)
                last.then_inc(o_done, 1)

            def add_out(t, g, s, first):
                pe.wait_ge(o_lo, g + 1)
                if s == 0 and not first:
                    pe.wait_ge(y_ready, KC * t)
                for m in range(KC):
                    for i, (a, c) in enumerate(PASSES):
                        last = nc.tensor.matmul(ps_y[m][:], wo(a, s, slice(m * P, (m + 1) * P)), oT[:, s % 2, c, :],
                                                start=(s == 0 and i == 0), stop=(s == HP - 1 and i == 2))
                    if s == HP - 1:
                        last.then_inc(y_done, 1)

            def project_first(h):
                if h == 0:
                    pe.wait_ge(ffn.y_lo, 1)
                    for n in range(ffn.AFTER_V, ffn.AFTER_QK):
                        pe.wait_ge(ffn.w_lo[n], 1)
                    pe.wait_ge(v_ready, PAIRS)
                else:
                    pe.wait_ge(ffn.res1_ready, 1)
                ffn.project_half(nc, 0, 0, h, ps_v)

            def tile(t):
                zero = isinstance(t, int) and t == 0
                for s in range(HP):
                    g = pair(t, s)
                    if exists(t, s + 2):
                        project_qk(g + 2, (s + 2) % HP, (k_ready, q_ready) if zero and s == 0 else (t1_ready, t0_ready),
                                   2 if zero and s == 0 else g, t + 1 if s + 2 == HP else None)
                    if exists(t, s + 1):
                        make_scores(g + 1, s + 1, False)
                    if exists(t, s - 1):
                        weigh_v(g - 1, (s - 1) % HP, pair(t, BLK) if 1 <= s <= BLK else
                                pair(t, 2 * BLK) if s else pair(t, 0), zero and s == 1)
                    if is_last(t) and s >= PROJECT_STEP:
                        project_first(s - PROJECT_STEP)
                    transpose_probs(g, s, g + 3 if exists(t, s + 2) else PAIRS)
                    if s < BLK or exists(t, HP):
                        if s == BLK:
                            pe.wait_ge(c_lo, 3 * (t + 1) + 1)
                        project_v(*v_group(t, s))
                    if zero and s == 2:
                        pe.wait_ge(w_lo, attn.WO + 1)
                    if exists(t, s - 2):
                        add_out(t if s >= 2 else t - 1, g - 2, (s - 2) % HP, zero)

            pe.wait_ge(w_lo, attn.WK + 1)
            pe.wait_ge(c_lo, 3)
            project_v(0, 0, slice(0, ST))
            project_qk(0, 0)
            project_v(1, 1, slice(0, ST))
            project_qk(1, 1, (k_ready, q_ready), 1)
            pe.wait_ge(k_zeroed, 4)
            make_scores(0, 0, True)
            for b in range(2, BLK):
                project_v(b, b, slice(0, ST))
            pe.wait_ge(attn.masks, 2)
            tiles(pe, tile)
            weigh_v(PAIRS - 1, HP - 1, pair(NST, 0), False)
            for g in (PAIRS - 2, PAIRS - 1):
                add_out(NST - 1, g, g % HP, False)


def ffn_phase(nc, x, yT, attn, ffn, b_base, b_thr, out):
    with ExitStack() as ctx:
        def sb(name, shape, dt):
            return ctx.enter_context(nc.sbuf_tensor(name, shape, dt))

        def psum(name):
            return ctx.enter_context(nc.psum_tensor(name, [P, ST], F32))

        def sem(name):
            return ctx.enter_context(nc.semaphore(name))

        wp, wf, wb = ffn.wp, ffn.wf, ffn.wb
        pb, bb = ffn.pb, sb("base_b_rows", [P, DM], F32)
        bt = sb("thr_b", [P, 2], F32)
        ident = attn.ident
        xt, yr, ys = ffn.xt, ffn.yr, ffn.ys
        x1 = [ffn.first_x1, sb("x1_odd", [P, DM], F32)]
        x1b = sb("x1_plus_bias", [P, 2, DM], F32)
        x1T = ffn.x1T
        res = sb("residual_sum", [P, 2, DM], F32)
        ot = sb("out_tile", [P, 2, DM], F32)
        hg = sb("h_and_gate", [P, LAST - P], F32)
        ngm = sb("gate_neg_max", [P, 1], F32)
        ge = sb("gate_exp", [P, EXPERTS], F32)
        den = sb("gate_denominators", [P, 2], F32)
        inv = sb("gate_inverses", [P, 2], F32)
        adapted = sb("gate_adapted", [P, EXPERTS], F32)
        wts = sb("gate_weights", [P, EXPERTS], F32)
        wsum = sb("gate_sum", [P, 3], F32)
        hw = sb("h_weighted", [P, ER], F32)
        hT = sb("h_weighted_T", [P, 2, P], F32R)
        ps_a = [psum("ps_a0"), psum("ps_a1")]
        ps_f = [[psum(f"ps_f{i}{n}") for n in range(3)] for i in range(2)]
        HT0 = LAST

        bias_loaded, bt_ready = sem("ffn_bias_loaded"), sem("thr_b_negated")
        x_loaded, y_loaded = ffn.x_loaded, ffn.y_loaded
        xb_ready, y_hi, y_lo = ffn.xb_ready, ffn.y_hi, ffn.y_lo
        proj_done, res1_ready, x1_ready = ffn.proj_done, ffn.res1_ready, ffn.x1_ready
        res2_ready = sem("res2_ready")
        x1b_ready = sem("x1b_ready")
        xT_done, xT_hi, xT_lo = sem("x1T_done"), sem("x1T_hi"), sem("x1T_lo")
        gate_done = sem("gate_done")
        base_done = sem("moe_done")
        hg_ready, ngm_ready, ge_ready = sem("h_gate_ready"), sem("gate_max_ready"), sem("gate_exp_ready")
        gate_step = sem("gate_step")
        hw_ready, hT_done = sem("h_weighted_ready"), sem("h_weighted_T_done")
        hT_hi, hT_lo = sem("h_weighted_T_hi"), sem("h_weighted_T_lo")
        out_ready = sem("out_ready")
        stored = [sem(f"out_stored{i}") for i in range(2)]

        block = ctx.enter_context(nc.Block())
        GATE_STEPS = 7

        def windows(eng, window):
            for i in range(4):
                window(i, i % 2, i)
            with eng.Fori(2, NBLK // 2 - 2) as m:
                for par in range(2):
                    window(2 * m + par, par, None)
            for i in range(NBLK - 4, NBLK):
                window(i, i % 2, i)

        def last(n, d):
            return n is not None and n + d >= NBLK

        @block.sync
        def _(sp):
            def load(i, par):
                sp.wait_ge(res1_ready, 2 * i - 2)
                sp.dma_start(xt[:, par, :], x[i]).then_inc(x_loaded[par], 16)
                sp.wait_ge(y_lo, i - 1)
                sp.dma_start(yr[:, par, :, :], yT[i]).then_inc(y_loaded[par], 16)

            def store(i, par):
                sp.wait_ge(out_ready, i + 1)
                sp.dma_start(out[i], ot[:, par, :]).then_inc(stored[par], 16)

            def window(i, par, n):
                if not last(n, 3):
                    load(i + 3, 1 - par)
                if n != 0:
                    store(i - 1, 1 - par)

            for b, src in ((bb[:], b_base), (bt[:, 0:1], b_thr)):
                sp.dma_start(b, src.partition_broadcast(P)).then_inc(bias_loaded, 16)
            sp.wait_ge(ffn.attn_stored, 16 * (UNITS + NST))
            load(2, 0)
            windows(sp, window)
            store(NBLK - 1, 1)
            for par in range(2):
                sp.wait_ge(stored[par], 16 * (NBLK // 2))

        @block.gpsimd
        def _(pool):
            def add_proj_b(i, par):
                pool.wait_ge(x_loaded[par], 8 * (i - par) + 16)
                nc.gpsimd.tensor_tensor(xt[:, par, :], xt[:, par, :], pb[:], ALU.add).then_inc(xb_ready, 1)

            def add_base_b(i, par, reuse):
                pool.wait_ge(x1_ready, i + 1)
                if reuse:
                    pool.wait_ge(res2_ready, 3 * (i - 1))
                nc.gpsimd.tensor_tensor(x1b[:, par, :], x1[par][:], bb[:], ALU.add).then_inc(x1b_ready, 1)

            def window(i, par, n):
                if not last(n, 1):
                    ffn.inverse_root(nc, pool, i + 1, 0)
                if not last(n, 2):
                    add_proj_b(i + 2, par)
                if n != 0:
                    ffn.inverse_root(nc, pool, i - 1, 1)
                if not last(n, 1):
                    add_base_b(i + 1, 1 - par, n != 0)

            _, dst, cols = ffn.weights[ffn.KEPT]
            pool.wait_ge(ffn.w_hi, ffn.KEPT + 1)
            nc.gpsimd.tensor_tensor(dst[:, LO, :], ffn.stage[ffn.KEPT % STAGES][:, 0:cols], dst[:, HI, :].bitcast(F32),
                                    ALU.subtract).then_inc(ffn.w_lo[ffn.KEPT], 1)
            pool.wait_ge(bias_loaded, 32)
            add_base_b(0, 0, False)
            windows(pool, window)
            ffn.inverse_root(nc, pool, NBLK - 1, 1)

        @block.scalar
        def _(act):
            def split_y(i, par):
                act.wait_ge(y_loaded[par], 8 * (i - par) + 16)
                act.wait_ge(proj_done, 2 * (i - 1))
                nc.scalar.activation(ys[:, par, HI, :, :], yr[:, par, :, :], ACT.Copy).then_inc(y_hi, 1)

            def gate_exps(i):
                act.wait_ge(ngm_ready, i + 1)
                nc.scalar.activation(ge[:], hg[:, ER:ER + EXPERTS], ACT.Exp, bias=ngm[:, 0:1],
                                     accum_out=den[:, 0:1]).then_inc(ge_ready, 1)
                nc.scalar.activation(den[:, 1:2], hg[:, ER + EXPERTS:ER + EXPERTS + 1], ACT.Exp, scale=-1.0,
                                     bias=bt[:, 1:2]).then_inc(ge_ready, 1)

            def split_hT(i, par):
                act.wait_ge(hT_done, i + 1)
                nc.scalar.activation(hT[:, HI, :], ps_f[par][2][:, HT0:HT0 + P], ACT.Copy).then_inc(hT_hi, 1)

            def split_xT(i, par):
                for h in range(2):
                    act.wait_ge(xT_done, 2 * i + h + 1)
                    nc.scalar.activation(x1T[:, par, HI, 4 * h:4 * h + 4, :], ps_a[h][:], ACT.Copy).then_inc(xT_hi, 1)

            def window(i, par, n):
                if not last(n, 2):
                    split_y(i + 2, par)
                gate_exps(i)
                if not last(n, 1):
                    split_xT(i + 1, 1 - par)
                split_hT(i, par)

            def split_late(n):
                _, dst, cols = ffn.weights[n]
                act.wait_ge(ffn.w_loaded[n % STAGES], 16 * (n // STAGES + 1))
                nc.scalar.activation(dst[:, HI, :], ffn.stage[n % STAGES][:, 0:cols], ACT.Copy).then_inc(ffn.w_hi, 1)

            split_late(ffn.KEPT)
            split_xT(0, 0)
            split_late(ffn.KEPT + 1)
            act.wait_ge(bias_loaded, 32)
            nc.scalar.mul(bt[:, 1:2], bt[:, 0:1], -1.0).then_inc(bt_ready, 1)
            act.wait_ge(bt_ready, 1)
            windows(act, window)

        @block.vector
        def _(dve):
            def first_norm(i, par, reuse, banks=ps_a):
                for h in range(2):
                    ffn.add_half(nc, dve, i, par, h, banks[h], res[:, 0, :])
                dve.wait_ge(res1_ready, 2 * i + 2)
                if reuse:
                    dve.wait_ge(xT_done, 2 * i - 2)
                    dve.wait_ge(x1b_ready, i - 1)
                ffn.ln_stats(nc, dve, i, 0, res[:, 0, :])
                ffn.ln_apply(nc, dve, i, 0, res[:, 0, :], x1[par][:], x1_ready)

            def second_sum(i, par):
                if not (isinstance(i, int) and i == 0):
                    dve.wait_ge(out_ready, i)
                dve.wait_ge(x1b_ready, i + 1)
                dve.wait_ge(base_done, i + 1)
                for n, (a, b) in enumerate(BANKS):
                    b = min(b, DM)
                    nc.vector.tensor_tensor(res[:, 1, a:b], ps_f[par][n][:, 0:b - a], x1b[:, par, a:b],
                                            ALU.add).then_inc(res2_ready, 1)
                dve.wait_ge(res2_ready, 3 * i + 3)
                ffn.ln_stats(nc, dve, i, 1, res[:, 1, :])

            def second_norm(i, par, reuse):
                if reuse:
                    dve.wait_ge(stored[par], 8 * (i - par))
                ffn.ln_apply(nc, dve, i, 1, res[:, 1, :], ot[:, par, :], out_ready)

            def split_y(i, par):
                dve.wait_ge(y_hi, i + 1)
                nc.vector.tensor_tensor(ys[:, par, LO, :, :], yr[:, par, :, :], ys[:, par, HI, :, :].bitcast(F32),
                                        ALU.subtract).then_inc(y_lo, 1)

            def gate(i, par):
                base = GATE_STEPS * i
                dve.wait_ge(gate_done, i + 1)
                nc.vector.tensor_copy(hg[:], ps_f[par][2][:, P:LAST]).then_inc(hg_ready, 1)
                dve.wait_ge(hg_ready, i + 1)
                nc.vector.tensor_reduce(ngm[:], hg[:, ER:ER + EXPERTS], AX_X, ALU.max, negate=True).then_inc(ngm_ready, 1)
                dve.wait_ge(ge_ready, 2 * i + 2)
                nc.vector.tensor_scalar(den[:, 1:2], den[:, 1:2], 1.0, 1.0 / MAX_THRESHOLD, ALU.add,
                                        ALU.mult).then_inc(gate_step, 1)
                dve.wait_ge(gate_step, base + 1)
                nc.vector.reciprocal(inv[:], den[:]).then_inc(gate_step, 1)
                dve.wait_ge(gate_step, base + 2)
                nc.vector.tensor_scalar(adapted[:], ge[:], inv[:, 0:1], inv[:, 1:2], ALU.mult,
                                        ALU.subtract).then_inc(gate_step, 1)
                dve.wait_ge(gate_step, base + 3)
                nc.vector.tensor_scalar(wts[:], adapted[:], 0.0, None, ALU.max).then_inc(gate_step, 1)
                dve.wait_ge(gate_step, base + 4)
                nc.vector.tensor_reduce(wsum[:, 0:1], wts[:], AX_X, ALU.add).then_inc(gate_step, 1)
                dve.wait_ge(gate_step, base + 5)
                nc.vector.scalar_tensor_tensor(out=wsum[:, 1:2], in0=wsum[:, 0:1], scalar=0.0, in1=wsum[:, 0:1],
                                               op0=ALU.is_equal, op1=ALU.add).then_inc(gate_step, 1)
                dve.wait_ge(gate_step, base + 6)
                nc.vector.reciprocal(wsum[:, 2:3], wsum[:, 1:2]).then_inc(gate_step, 1)
                dve.wait_ge(gate_step, base + 7)
                nc.vector.scalar_tensor_tensor(
                    out=hw[:].rearrange("p (e r) -> p e r", e=EXPERTS),
                    in0=hg[:, 0:ER].rearrange("p (e r) -> p e r", e=EXPERTS), scalar=wsum[:, 2:3],
                    in1=wts[:].unsqueeze(2).broadcast_to([P, EXPERTS, RANK]),
                    op0=ALU.mult, op1=ALU.mult).then_inc(hw_ready, 1)

            def split_hT(i, par):
                dve.wait_ge(hT_hi, i + 1)
                nc.vector.tensor_tensor(hT[:, LO, :], ps_f[par][2][:, HT0:HT0 + P], hT[:, HI, :].bitcast(F32),
                                        ALU.subtract).then_inc(hT_lo, 1)

            def split_xT(i, par):
                for h in range(2):
                    dve.wait_ge(xT_hi, 2 * i + h + 1)
                    part = slice(4 * h, 4 * h + 4)
                    nc.vector.tensor_tensor(x1T[:, par, LO, part, :], ps_a[h][:].rearrange("p (c n) -> p c n", c=4),
                                            x1T[:, par, HI, part, :].bitcast(F32), ALU.subtract).then_inc(xT_lo, 1)

            def window(i, par, n):
                if not last(n, 1):
                    first_norm(i + 1, 1 - par, n != 0, ps_f[1] if n == 0 else ps_a)
                if not last(n, 2):
                    split_y(i + 2, par)
                gate(i, par)
                if n != 0:
                    second_sum(i - 1, 1 - par)
                if not last(n, 1):
                    split_xT(i + 1, 1 - par)
                split_hT(i, par)
                if n != 0:
                    second_norm(i - 1, 1 - par, n is None or n >= 3)

            def split_late(n):
                _, dst, cols = ffn.weights[n]
                dve.wait_ge(ffn.w_hi, n + 1)
                nc.vector.tensor_tensor(dst[:, LO, :], ffn.stage[n % STAGES][:, 0:cols], dst[:, HI, :].bitcast(F32),
                                        ALU.subtract).then_inc(ffn.w_lo[n], 1)

            split_xT(0, 0)
            split_late(len(ffn.weights) - 1)
            windows(dve, window)
            second_sum(NBLK - 1, 1)
            second_norm(NBLK - 1, 1, True)

        @block.tensor
        def _(pe):
            def project(i, par, banks=ps_a):
                pe.wait_ge(y_lo, i + 1)
                if not (isinstance(i, int) and i < 2):
                    pe.wait_ge(xT_lo, 2 * i)
                for h in range(2):
                    ffn.project_half(nc, i, par, h, banks[h])

            def transpose_x1(i, par):
                pe.wait_ge(x1_ready, i + 1)
                for h in range(2):
                    for c in range(4):
                        mm = nc.tensor.transpose(ps_a[h][:, c * P:(c + 1) * P],
                                                 x1[par][:, (4 * h + c) * P:(4 * h + c + 1) * P], ident[:])
                    mm.then_inc(xT_done, 1)

            def base(i, par, n, kcs):
                a0, b0 = BANKS[n]
                for kc in kcs:
                    if n == 2 and isinstance(i, int) and i == 0 and kc >= CC - ffn.LATE:
                        pe.wait_ge(ffn.w_lo[ffn.KEPT + kc - (CC - ffn.LATE)], 1)
                    for k, (a, b) in enumerate(PASSES):
                        mm = nc.tensor.matmul(ps_f[par][n][:, 0:b0 - a0], x1T[:, par, a, kc, :], wf[kc][:, b, a0:b0],
                                              start=(kc == 0 and k == 0), stop=(n == 2 and kc == CC - 1 and k == 2),
                                              skip_group_check=True)
                if n == 2:
                    mm.then_inc(gate_done, 1)

            def transpose_h(i, par):
                pe.wait_ge(hw_ready, i + 1)
                nc.tensor.matmul(ps_f[par][2][:, HT0:HT0 + P], hw[:], ident[:], is_transpose=True, start=False,
                                 stop=True, skip_group_check=True).then_inc(hT_done, 1)

            def experts(i, par):
                pe.wait_ge(hT_lo, i + 1)
                for n, (a0, b0) in enumerate(BANKS):
                    b0 = min(b0, DM)
                    for k, (a, b) in enumerate(PASSES):
                        mm = nc.tensor.matmul(ps_f[par][n][:, 0:b0 - a0], hT[:, a, :], wb[:, b, a0:b0],
                                              start=False, stop=(k == 2), skip_group_check=True)
                mm.then_inc(base_done, 1)

            def window(i, par, n):
                pe.wait_ge(xT_lo, 2 * i + 2)
                if n is None or n >= 2:
                    pe.wait_ge(res2_ready, 3 * (i - 1))
                base(i, par, 2, range(CC))
                base(i, par, 0, range(CC))
                if not last(n, 1):
                    transpose_x1(i + 1, 1 - par)
                base(i, par, 1, range(CC // 2))
                transpose_h(i, par)
                base(i, par, 1, range(CC // 2, CC))
                experts(i, par)
                if not last(n, 2):
                    project(i + 2, par)

            transpose_x1(0, 0)
            project(1, 1, ps_f[1])
            for n in range(ffn.KEPT):
                pe.wait_ge(ffn.w_lo[n], 1)
            windows(pe, window)


def build(nc, ins, out):
    convT = nc.dram_tensor("convT_scratch", [2 * NST, P, CF // 2, ST], F32).ap()
    yT = nc.dram_tensor("yT_scratch", [P, KC, TOK], F32).ap()
    with ExitStack() as ctx:
        attn = AttentionStart(ctx, nc)
        conv_phase(nc, ins["xT"], ins["conv_w"], ins["conv_b"], convT, attn, ins["attn_w"], ins["q_bias"],
                   ins["k_bias"], ins["v_bias"], ins["o_bias"])
        ffn = FfnStart(ctx, nc, attn, ins["proj_w"], ins["ffn_w"], ins["lora_b"])
        attention_phase(nc, convT, attn, TileColumns(yT, ST), ffn, ins["x"], TileColumns(yT, P), ins["proj_b"])
        ffn_phase(nc, ins["x"], TileColumns(yT, P), attn, ffn, ins["b_base"], ins["b_thr"], out)


class TileColumns:

    def __init__(self, ap, width):
        self.ap, self.width = ap, width

    def __getitem__(self, t):
        return self.ap[:, :, bass.ds(t * self.width, self.width)]


def kernel(**inputs):
    import concourse.bacc as bacc
    from concourse.bass_utils import run_bass_kernel_spmd

    a = {k: np.asarray(v) for k, v in inputs.items()}
    x = a["L0_attn_inputs"]
    padded = np.zeros((BATCH, DM, SEQ + TAPS - 1), x.dtype)
    padded[:, :, 1:SEQ + 1] = x.transpose(0, 2, 1)
    xT = np.stack([padded[t // ST_SEQ, :, (t % ST_SEQ) * ST:(t % ST_SEQ) * ST + WIN] for t in range(NST)])

    def chunks(w):
        return w.reshape(-1, P, w.shape[-1]).transpose(1, 0, 2)

    def columns(b):
        return b.reshape(-1, P).T

    w_in = [chunks(a[f"L0_attn_w{n}"].reshape(WB, HE)) for n in "vqk"]
    attn_w = np.stack([w.reshape(P, -1) for w in w_in + [chunks(a["L0_attn_wo"].reshape(HE, WB))]])
    ffn_w = np.concatenate([a["L0_ffn_W_base"], a["L0_ffn_A"].reshape(ER, DM), a["L0_ffn_W_gate"],
                            a["L0_ffn_W_thr"], np.zeros((1, DM), x.dtype)]).T
    arrays = {
        "xT": xT.reshape(NST, CC, P, WIN // 2, 2).swapaxes(3, 4),
        "conv_w": a["L0_attn_conv_w"].reshape(TAPS, CC, P, 2, 3 * WB // 2).transpose(3, 1, 2, 0, 4),
        "conv_b": columns(a["L0_attn_conv_b"]),
        "attn_w": attn_w,
        "q_bias": columns(a["L0_attn_bq"]),
        "k_bias": columns(a["L0_attn_bk"]),
        "v_bias": a["L0_attn_bv"].reshape(HE),
        "o_bias": columns(a["L0_attn_bo"]),
        "x": x.reshape(NBLK, P, DM),
        "proj_w": a["L0_attn_proj_w"].reshape(KC, P, DM),
        "proj_b": a["L0_attn_proj_b"],
        "ffn_w": ffn_w.reshape(CC, P, WCOLS),
        "lora_b": a["L0_ffn_B"].transpose(0, 2, 1).reshape(ER, DM),
        "b_base": a["L0_ffn_b_base"],
        "b_thr": a["L0_ffn_b_thr"],
    }
    arrays = {k: np.ascontiguousarray(v) for k, v in arrays.items()}
    nc = bacc.Bacc("TRN2", target_bir_lowering=False, num_devices=1)
    ins = {k: nc.dram_tensor(f"in_{k}", v.shape, mybir.dt.from_np(v.dtype), kind="ExternalInput").ap() for k, v in arrays.items()}
    out = nc.dram_tensor("out", [NBLK, P, DM], F32, kind="ExternalOutput").ap()
    build(nc, ins, out)
    result = run_bass_kernel_spmd(nc, [{f"in_{k}": v for k, v in arrays.items()}], core_ids=[0])
    return result.results[0]["out"].reshape(BATCH, SEQ, DM)
```
